# Optimizing a Trainium2 kernel written in Bass

```python
import numpy as np
import jax
import jax.numpy as jnp

def _softmax(x, axis=-1):
    return jax.nn.softmax(x, axis=axis)
def _gelu(x):
    return jax.nn.gelu(x, approximate=True)
def _silu(x):
    return jax.nn.silu(x)
def _sigmoid(x):
    return jax.nn.sigmoid(x)
def _layernorm(x, axis=-1, eps=1e-5):
    m = jnp.mean(x, axis=axis, keepdims=True)
    v = jnp.var(x, axis=axis, keepdims=True)
    return (x - m) / jnp.sqrt(v + eps)
def _scatter_add(tgt, idx, src, axis=0):
    return tgt.at[idx].add(src)
def _segment_sum(src, seg, n):
    return jax.ops.segment_sum(src, seg, n)

kernel_name = 'mk_adj_seq_d2_adj_256_5f9f59'

def setup_inputs(seed: int = 0):
    np.random.seed(seed)
    _w = jnp.asarray
    def _rec_inputs():
        import jax
        import jax.numpy as jnp
        _gk = jax.random.key(seed)
        x = -0.0005207 + 1.001 * jax.random.normal(jax.random.fold_in(_gk, 1), (64, 256, 256), jnp.float32)
        _w = (1.0 + jnp.arange(256, dtype=jnp.float32)) ** -0.5
        _w = _w / _w.mean()
        _pij = jnp.clip(0.015625 * _w[:, None] * _w[None, :], 0.0, 1.0)
        _a = jax.random.uniform(jax.random.fold_in(_gk, 2), (64, 256, 256)) < _pij
        _a = jnp.logical_or(_a, jnp.eye(256, dtype=bool))
        adj = _a.astype(jnp.int32)
        return x, adj
    x, adj = _rec_inputs()
    def _L0_gnn_setup():
        import jax, jax.numpy as jnp
        import numpy as np
        ALPHA = 0.2
        EPS = 1e-05
        NEG = -9000000000000000.0
        H, DH = (8, 32)

        def _layernorm(x, g, b):
            mu = jnp.mean(x, axis=-1, keepdims=True)
            var = jnp.mean(jnp.square(x - mu), axis=-1, keepdims=True)
            return (x - mu) * jax.lax.rsqrt(var + EPS) * g + b
        key = jax.random.key(seed)
        ks = jax.random.split(key, 6)
        w, n, d = (4, 2048, 256)
        feats = jax.random.normal(ks[0], (w, n, d), dtype=jnp.float32)
        adj = jax.random.randint(ks[1], (w, n, n), 0, 2, dtype=jnp.int32)
        adj = adj.at[:, jnp.arange(n), jnp.arange(n)].set(1)
        s = 0.06
        Wq = jax.random.normal(ks[2], (d, H * DH), dtype=jnp.float32) * s
        Wk = jax.random.normal(ks[3], (d, H * DH), dtype=jnp.float32) * s
        Wv = jax.random.normal(ks[4], (d, H * DH), dtype=jnp.float32) * s
        Wffn = jax.random.normal(ks[5], (H * DH, H * DH + d), dtype=jnp.float32) * 0.05
        g1 = jnp.ones((H * DH,), jnp.float32)
        b1 = jnp.zeros((H * DH,), jnp.float32)
        g2 = jnp.ones((H * DH,), jnp.float32)
        b2 = jnp.zeros((H * DH,), jnp.float32)
        return {'features': feats, 'adj': adj, 'Wq': Wq, 'Wk': Wk, 'Wv': Wv, 'Wffn': Wffn, 'g1': g1, 'b1': b1, 'g2': g2, 'b2': b2}
    _L0_gnn_all = _L0_gnn_setup()
    _L0_gnn_in = {k: v for k, v in _L0_gnn_all.items() if k in ('Wq', 'Wk', 'Wv', 'Wffn', 'g1', 'b1', 'g2', 'b2', )}
    del _L0_gnn_all

    def _L1_gnn_setup():
        import jax, jax.numpy as jnp
        import numpy as np
        B, N, D = (8, 1024, 256)
        H = 8
        DH = D // H
        R = 4
        FF = 1024
        EPS = 1e-05

        def _lin(k, fan_in, shape):
            return jax.random.normal(k, shape, jnp.float32) * (1.0 / np.sqrt(fan_in))

        def _ln(x, g, b):
            m = x.mean(-1, keepdims=True)
            v = ((x - m) ** 2).mean(-1, keepdims=True)
            return (x - m) * jax.lax.rsqrt(v + EPS) * g + b
        key = jax.random.key(seed)
        ks = jax.random.split(key, 16)
        src = jax.random.normal(ks[0], (B, N, D), jnp.float32)
        adj_matrix = jax.random.randint(ks[1], (B, N, N), 0, 5, dtype=jnp.int32)
        Wq = _lin(ks[2], D, (D, D))
        bq = jnp.zeros((D,), jnp.float32)
        Wk = _lin(ks[3], D, (D, D))
        bk = jnp.zeros((D,), jnp.float32)
        Wv = _lin(ks[4], D, (R, D, D))
        bv = jnp.zeros((R, D), jnp.float32)
        Wo = _lin(ks[5], D, (D, D))
        bo = jnp.zeros((D,), jnp.float32)
        W1 = _lin(ks[6], D, (D, FF))
        b1 = jnp.zeros((FF,), jnp.float32)
        W2 = _lin(ks[7], FF, (FF, D))
        b2 = jnp.zeros((D,), jnp.float32)
        g1 = jnp.ones((D,), jnp.float32)
        beta1 = jnp.zeros((D,), jnp.float32)
        g2 = jnp.ones((D,), jnp.float32)
        beta2 = jnp.zeros((D,), jnp.float32)
        return dict(src=src, adj_matrix=adj_matrix, Wq=Wq, bq=bq, Wk=Wk, bk=bk, Wv=Wv, bv=bv, Wo=Wo, bo=bo, W1=W1, b1=b1, W2=W2, b2=b2, g1=g1, beta1=beta1, g2=g2, beta2=beta2)
    _L1_gnn_all = _L1_gnn_setup()
    _L1_gnn_in = {k: v for k, v in _L1_gnn_all.items() if k in ('Wq', 'bq', 'Wk', 'bk', 'Wv', 'bv', 'Wo', 'bo', 'W1', 'b1', 'W2', 'b2', 'g1', 'beta1', 'g2', 'beta2', )}
    del _L1_gnn_all

    return {
        "x": x,
        "adj": adj,
        "L0_gnn_Wq": _L0_gnn_in["Wq"],
        "L0_gnn_Wk": _L0_gnn_in["Wk"],
        "L0_gnn_Wv": _L0_gnn_in["Wv"],
        "L0_gnn_Wffn": _L0_gnn_in["Wffn"],
        "L0_gnn_g1": _L0_gnn_in["g1"],
        "L0_gnn_b1": _L0_gnn_in["b1"],
        "L0_gnn_g2": _L0_gnn_in["g2"],
        "L0_gnn_b2": _L0_gnn_in["b2"],
        "L1_gnn_Wq": _L1_gnn_in["Wq"],
        "L1_gnn_bq": _L1_gnn_in["bq"],
        "L1_gnn_Wk": _L1_gnn_in["Wk"],
        "L1_gnn_bk": _L1_gnn_in["bk"],
        "L1_gnn_Wv": _L1_gnn_in["Wv"],
        "L1_gnn_bv": _L1_gnn_in["bv"],
        "L1_gnn_Wo": _L1_gnn_in["Wo"],
        "L1_gnn_bo": _L1_gnn_in["bo"],
        "L1_gnn_W1": _L1_gnn_in["W1"],
        "L1_gnn_b1": _L1_gnn_in["b1"],
        "L1_gnn_W2": _L1_gnn_in["W2"],
        "L1_gnn_b2": _L1_gnn_in["b2"],
        "L1_gnn_g1": _L1_gnn_in["g1"],
        "L1_gnn_beta1": _L1_gnn_in["beta1"],
        "L1_gnn_g2": _L1_gnn_in["g2"],
        "L1_gnn_beta2": _L1_gnn_in["beta2"],
    }

def reference(x, adj, L0_gnn_Wq, L0_gnn_Wk, L0_gnn_Wv, L0_gnn_Wffn, L0_gnn_g1, L0_gnn_b1, L0_gnn_g2, L0_gnn_b2, L1_gnn_Wq, L1_gnn_bq, L1_gnn_Wk, L1_gnn_bk, L1_gnn_Wv, L1_gnn_bv, L1_gnn_Wo, L1_gnn_bo, L1_gnn_W1, L1_gnn_b1, L1_gnn_W2, L1_gnn_b2, L1_gnn_g1, L1_gnn_beta1, L1_gnn_g2, L1_gnn_beta2):
    import jax
    import jax.numpy as jnp
    def _L0_gnn_ref(features, adj, Wq, Wk, Wv, Wffn, g1, b1, g2, b2):
        import jax, jax.numpy as jnp
        import numpy as np
        ALPHA = 0.2
        EPS = 1e-05
        NEG = -9000000000000000.0
        H, DH = (8, 32)

        def _layernorm(x, g, b):
            mu = jnp.mean(x, axis=-1, keepdims=True)
            var = jnp.mean(jnp.square(x - mu), axis=-1, keepdims=True)
            return (x - mu) * jax.lax.rsqrt(var + EPS) * g + b
        w, n, d = features.shape

        def heads(x):
            return x.reshape(w, n, H, DH).transpose(0, 2, 1, 3)
        q = heads(features @ Wq)
        k = heads(features @ Wk)
        v = heads(features @ Wv)
        e = jnp.einsum('whqd,whkd->whqk', q, k)
        e = jnp.where(e >= 0, e, ALPHA * e)
        attn = jax.nn.softmax(jnp.where(adj[:, None] > 0, e, NEG), axis=-1)
        h = jnp.einsum('whqk,whkd->whqd', attn, v)
        h = h.transpose(0, 2, 1, 3).reshape(w, n, H * DH)
        out = _layernorm(h, g1, b1)
        out = jnp.concatenate([out, features], axis=-1) @ Wffn.T
        out = _layernorm(out, g2, b2)
        return out + features

    def _L1_gnn_ref(src, adj_matrix, Wq, bq, Wk, bk, Wv, bv, Wo, bo, W1, b1, W2, b2, g1, beta1, g2, beta2):
        import jax, jax.numpy as jnp
        import numpy as np
        B, N, D = (8, 1024, 256)
        H = 8
        DH = D // H
        R = 4
        FF = 1024
        EPS = 1e-05

        def _lin(k, fan_in, shape):
            return jax.random.normal(k, shape, jnp.float32) * (1.0 / np.sqrt(fan_in))

        def _ln(x, g, b):
            m = x.mean(-1, keepdims=True)
            v = ((x - m) ** 2).mean(-1, keepdims=True)
            return (x - m) * jax.lax.rsqrt(v + EPS) * g + b
        Bb, Nn, Dm = src.shape
        h, dh = (H, Dm // H)
        q = (src @ Wq + bq).reshape(Bb, Nn, h, dh).transpose(0, 2, 1, 3)
        k = (src @ Wk + bk).reshape(Bb, Nn, h, dh).transpose(0, 2, 1, 3)
        scores = jnp.einsum('bhid,bhjd->bhij', q, k) / np.sqrt(dh)
        attn = jax.nn.softmax(scores, axis=-1)
        out = jnp.zeros_like(q)
        for r in range(Wv.shape[0]):
            v_r = (src @ Wv[r] + bv[r]).reshape(Bb, Nn, h, dh).transpose(0, 2, 1, 3)
            mask = (adj_matrix == r)[:, None]
            out = out + jnp.einsum('bhij,bhjd->bhid', attn * mask, v_r)
        attn_out = out.transpose(0, 2, 1, 3).reshape(Bb, Nn, Dm) @ Wo + bo
        x = _ln(src + attn_out, g1, beta1)
        ff = jax.nn.gelu(x @ W1 + b1, approximate=False) @ W2 + b2
        return _ln(x + ff, g2, beta2)

    x = _L0_gnn_ref(x, adj, L0_gnn_Wq, L0_gnn_Wk, L0_gnn_Wv, L0_gnn_Wffn, L0_gnn_g1, L0_gnn_b1, L0_gnn_g2, L0_gnn_b2)
    x = _L1_gnn_ref(x, adj, L1_gnn_Wq, L1_gnn_bq, L1_gnn_Wk, L1_gnn_bk, L1_gnn_Wv, L1_gnn_bv, L1_gnn_Wo, L1_gnn_bo, L1_gnn_W1, L1_gnn_b1, L1_gnn_W2, L1_gnn_b2, L1_gnn_g1, L1_gnn_beta1, L1_gnn_g2, L1_gnn_beta2)
    return x


_drawn_inputs = setup_inputs


def setup_inputs(seed=0):
    import zlib

    import numpy as np

    out = dict(_drawn_inputs(seed))
    spreads = {'L0_gnn_g1': (1.0, 0.2),
     'L0_gnn_b1': (0.0, 0.1),
     'L0_gnn_g2': (1.0, 0.2),
     'L0_gnn_b2': (0.0, 0.1),
     'L1_gnn_bq': (0.0, 0.269),
     'L1_gnn_bk': (0.0, 0.8),
     'L1_gnn_bv': (0.0, 0.1),
     'L1_gnn_bo': (0.0, 0.1),
     'L1_gnn_b1': (0.0, 0.1),
     'L1_gnn_b2': (0.0, 0.1),
     'L1_gnn_g1': (1.0, 0.2),
     'L1_gnn_beta1': (0.0, 0.1),
     'L1_gnn_g2': (1.0, 0.2),
     'L1_gnn_beta2': (0.0, 0.1)}
    factors = {}
    for name, (base, spread) in spreads.items():
        noise = np.random.default_rng([zlib.crc32(name.encode()), seed]).standard_normal(out[name].shape)
        drawn = base * np.exp(spread * noise) if base else spread * noise
        out[name] = jnp.asarray(drawn.astype(out[name].dtype))
    for name, factor in factors.items():
        out[name] = (out[name] * factor).astype(out[name].dtype)
    return out
```

```python
from contextlib import ExitStack

import concourse.bass as bass
from concourse import mybir

F32 = mybir.dt.float32
BF16 = mybir.dt.bfloat16
I32 = mybir.dt.int32
ALU = mybir.AluOpType
ACT = mybir.ActivationFunctionType
AX = mybir.AxisListType

P = 128
D = 256
N = 256
C = D // P
T = N // P
H, DH = 8, 32
Q = P // DH
R = 4
FF = 1024
FC = FF // P
FB = FC // 2
U = H * T // 2
NEG = -float(2 ** 53)
SLOPE = 0.2
EPS = 1e-5
BIG = 3e38
SCALE = float(DH) ** -0.5


def unit(u):
    return u // 4, 2 * (u % 4 // 2), u % 2


def later(n):
    return not (isinstance(n, int) and n == 0)


L1_HEAD = [("x1",), ("m1",), ("q1",), ("k1",), ("v1", 0), ("v1", 1), ("v1", 2), ("v1", 3)]


def units(layer):
    out = []
    for u in range(U):
        out.append([("S1", u)] if layer else [("R0", u), ("S0", u)])
        if u:
            out[-1].append(("T%d" % layer, u - 1))
            if u % 4 == 0:
                out[-1].append(("A%d" % layer, u // 4 - 1))
    out.append([("T%d" % layer, U - 1), ("A%d" % layer, 1)])
    return out


def make_order():
    u0, u1 = units(0), units(1)
    order = [("x0",), ("x1",), ("q0",), ("m1",), ("k0",), ("q1",), ("v0",), ("k1",)]
    order += u0[0] + [("v1", 0)] + u0[1] + [("v1", 1)] + u0[2] + [("v1", 2), ("v1", 3)]
    order += [("adj0",)]
    for k in range(9):
        order += u1[k]
        if k + 3 < 9:
            order += u0[k + 3]
        elif k == 6:
            order += [("O0",)]
        elif k == 7:
            order += [("N0",)]
        elif k == 8:
            order += [("F0",)]
    order += [("W1",), ("Y0",), ("X1",), ("F1", 0), ("F1", 1), ("F1", 2), ("F1", 3), ("F2",), ("Y1",)]
    return order


ORDER = make_order()


def graph_layers_kernel(nc, x, adj, w, out):
    G = x.shape[0]
    ctx = ExitStack()
    with ctx:
        def sb(name, shape, dt=F32):
            return ctx.enter_context(nc.sbuf_tensor(name, shape, dt))

        def bank(name):
            return ctx.enter_context(nc.psum_tensor(name, [P, 512], F32))

        def sem(name):
            return ctx.enter_context(nc.semaphore(name))

        ident = sb("ident", [P, P])
        identb = sb("identb", [P, P], BF16)
        wq0, wk0, wv0 = (sb(f"w{a}0_sb", [P, C, D]) for a in "qkv")
        wf0 = sb("wf0", [P, 2 * C, D])
        wq1, wk1, wo1 = (sb(f"w{a}1_sb", [P, C, D]) for a in "qko")
        wv1 = sb("wv1_sb", [P, R, C, D])
        w1 = sb("w1_sb", [P, C, FF])
        w2 = sb("w2_sb", [P, FC, D])
        rep = {name: sb(f"rep_{name}", [P, 1, D]) for name in
               ("L0_gnn_g2", "L0_gnn_b2", "L1_gnn_bo", "L1_gnn_g1", "L1_gnn_beta1", "L1_gnn_b2",
                "L1_gnn_g2", "L1_gnn_beta2")}
        bv = sb("bv_rep", [P, R, 1, D])
        col = {name: sb(f"col_{name}", [P, n]) for name, n in
               (("L0_gnn_g1", C), ("L0_gnn_b1", C), ("L1_gnn_bq", C), ("L1_gnn_bk", C), ("L1_gnn_b1", FC))}
        minus_half = sb("minus_half", [P, T])
        held = sb("held", [P, 1])
        bqs = sb("bqs", [P, C])

        x_in = sb("x_in", [P, T, D])
        adj_in = sb("adj_in", [P, T, N], I32)
        xb = sb("xb", [P, T, D])
        negm = sb("negm", [P, T, N], BF16)
        adjb = sb("adjb", [P, T, N], BF16)
        xT0 = sb("xT0", [P, C, N])
        qT0 = sb("qT0", [P, C, N])
        kP0 = sb("kP0", [P, H, N])
        V0 = sb("V0", [P, T, D])
        P0 = sb("P0", [P, 2, 2, N])
        PT0 = sb("PT0", [P, C, Q, T, N])
        nb0 = sb("nb0", [P, U, 2])
        sum0 = sb("sum0", [P, T, H])
        rinv0 = sb("rinv0", [P, T, H])
        oT0 = sb("oT0", [P, C, N])
        h0 = sb("h0", [P, T, D])
        z0 = sb("z0", [P, T, D])
        zf0 = sb("zf0", [P, C, N])
        y0 = sb("y0", [P, T, D])
        y0g = sb("y0g", [P, T, D])
        x1 = sb("x1", [P, T, D])
        x1b = sb("x1b", [P, T, D])
        xT1 = sb("xT1", [P, C, N])
        M1 = sb("M1", [P, R, T, N], BF16)
        qT1 = sb("qT1", [P, C, N])
        kP1 = sb("kP1", [P, H, N])
        V1 = sb("V1", [P, R, T, D])
        P1 = sb("P1", [P, 2, 2, N])
        A1 = sb("A1", [P, R, Q, T, N])
        nb1 = sb("nb1", [P, U, 2])
        sum1 = sb("sum1", [P, T, H])
        rinv1 = sb("rinv1", [P, T * H, 1])
        rsp1 = sb("rsp1", [P, T, D])
        oT1 = sb("oT1", [P, C, N])
        at1 = sb("at1", [P, C, N])
        r1 = sb("r1", [P, T, D])
        n1 = sb("n1", [P, T, D])
        n1g = sb("n1g", [P, T, D])
        x2 = sb("x2", [P, T, D])
        x2b = sb("x2b", [P, T, D])
        x2T = sb("x2T", [P, C, N])
        gT = sb("gT", [P, FC, N])
        wf0_in = gT[:, 0:4, :].rearrange("p (c a) n -> p c (a n)", c=C)
        r2 = sb("r2", [P, T, D])
        n2 = sb("n2", [P, T, D])
        out_tok = sb("out_tok", [P, T, D])
        ln = {k: (sb(f"st_{k}", [P, T, 6]), sb(f"mv_{k}", [P, T, 2]), sb(f"ve_{k}", [P, T]),
                  sb(f"rs_{k}", [P, T])) for k in ("a0", "b0", "a1", "b1")}
        ln_sem = {k: (sem(f"stats_{k}"), sem(f"moments_{k}"), sem(f"var_{k}_ready"), sem(f"rstd_{k}_ready"))
                  for k in ln}

        S0, G0, T0, O0 = bank("S0"), bank("G0"), bank("T0"), bank("O0")
        S1, G1, T1, O1 = bank("S1"), bank("G1"), bank("T1"), bank("O1")

        def two(b):
            return b[:, :].rearrange("p (a n) -> p a n", a=2)

        weights_loaded = sem("weights_loaded")
        cols_loaded = sem("cols_loaded")
        zeroed = sem("zeroed")
        ident_ready = sem("ident_ready")
        identb_ready = sem("identb_ready")
        half_ready = sem("half_ready")
        kpad_zeroed = sem("kpad_zeroed")
        bqs_ready = sem("bqs_ready")
        wfT_psum = sem("wfT_psum")
        wf_ready = sem("wf_ready")
        x_loaded, adj_loaded, out_stored = sem("x_loaded"), sem("adj_loaded"), sem("out_stored")
        xT0_psum, xT0_ready, xb_ready = sem("xT0_psum"), sem("xT0_ready"), sem("xb_ready")
        negm_ready, adjb_ready = sem("negm_ready"), sem("adjb_ready")
        q0_psum, q0_ready, k0_psum, k0_ready = sem("q0_psum"), sem("q0_ready"), sem("k0_psum"), sem("k0_ready")
        v0_psum, v0_ready = sem("v0_psum"), sem("v0_ready")
        scores0, relu0_ready = sem("scores0"), sem("relu0_ready")
        leaky0_ready, exp0_ready = sem("leaky0_ready"), sem("exp0_ready")
        pT0_psum, PT0_ready, av0_psum = sem("pT0_psum"), sem("PT0_ready"), sem("av0_psum")
        oT0_ready, o0_psum, rinv0_ready, h0_ready = sem("oT0_ready"), sem("o0_psum"), sem("rinv0_ready"), sem("h0_ready")
        z0_ready, zT0_psum, zf0_ready = sem("z0_ready"), sem("zT0_psum"), sem("zf0_ready")
        ffn0_psum, y0_ready, y0g_ready, x1_ready = sem("ffn0_psum"), sem("y0_ready"), sem("y0g_ready"), sem("x1_ready")
        xT1_psum, xT1_ready, x1b_ready = sem("xT1_psum"), sem("xT1_ready"), sem("x1b_ready")
        adjT_psum, mask_ready = sem("adjT_psum"), sem("mask_ready")
        q1_psum, q1_ready, k1_psum, k1_ready = sem("q1_psum"), sem("q1_ready"), sem("k1_psum"), sem("k1_ready")
        v1_psum, v1_ready = sem("v1_psum"), sem("v1_ready")
        scores1, bias1_ready, exp1_ready = sem("scores1"), sem("bias1_ready"), sem("exp1_ready")
        pT1_psum, A1_ready, av1_psum = sem("pT1_psum"), sem("A1_ready"), sem("av1_psum")
        oT1_ready, rinv1_ready, rsp1_ready, rT1_psum, at1_ready = sem("oT1_ready"), sem("rinv1_ready"), sem("rsp1_ready"), sem("rT1_psum"), sem("at1_ready")
        wo1_psum, r1_ready, n1_ready, n1g_ready = sem("wo1_psum"), sem("r1_ready"), sem("n1_ready"), sem("n1g_ready")
        x2_ready, x2b_ready, x2T_psum, x2T_ready = sem("x2_ready"), sem("x2b_ready"), sem("x2T_psum"), sem("x2T_ready")
        up_psum, gT_ready = sem("up_psum"), sem("gT_ready")
        down_psum, r2_ready, n2_ready, n2g_ready, out_ready = sem("down_psum"), sem("r2_ready"), sem("n2_ready"), sem("n2g_ready"), sem("out_ready")

        def chunks(a):
            return a.rearrange("(c p) o -> p c o", p=P)

        wide = [(wq0[:, :, :], chunks(w["L0_gnn_Wq"])), (wk0[:, :, :], chunks(w["L0_gnn_Wk"])),
                (wv0[:, :, :], chunks(w["L0_gnn_Wv"])), (wf0_in[:, :, :], chunks(w["L0_gnn_Wffn"])),
                (wq1[:, :, :], chunks(w["L1_gnn_Wq"])), (wk1[:, :, :], chunks(w["L1_gnn_Wk"])),
                (wo1[:, :, :], chunks(w["L1_gnn_Wo"])), (w1[:, :, :], chunks(w["L1_gnn_W1"])),
                (w2[:, :, :], chunks(w["L1_gnn_W2"]))]
        wide += [(wv1[:, r, :, :], chunks(w["L1_gnn_Wv"][r])) for r in range(R)]
        wide += [(rep[name][:, 0, :], w[name].partition_broadcast(P)) for name in rep]
        wide += [(bv[:, r, 0, :], w["L1_gnn_bv"][r].partition_broadcast(P)) for r in range(R)]
        narrow = [(col[name][:, :], w[name].rearrange("(c p) -> p c", p=P)) for name in col]
        x_v = x.rearrange("g (t p) d -> g p t d", p=P)
        adj_v = adj.rearrange("g (t p) m -> g p t m", p=P)
        out_v = out.rearrange("g (t p) d -> g p t d", p=P)

        def graph(view, n):
            if isinstance(n, int):
                return view[n]
            return view[bass.ds(n, 1)].rearrange("g p t d -> (g p) t d")

        def run_stages(stages, i, layers):
            for name, *k in ORDER:
                layer = int(name[-1]) if name != "F2" and name[0] != "F" else (0 if name == "F0" else 1)
                if layer in layers and name in stages:
                    stages[name](i - layer if layer else i, *k)

        def all_graphs(eng, stages):
            run_stages(stages, 0, (0,))
            run_stages(stages, 1, (0, 1))
            with eng.Fori(2, G) as i:
                run_stages(stages, i, (0, 1))
            run_stages(stages, G, (1,))

        block = ctx.enter_context(nc.Block())

        @block.sync
        def _(sp):
            sp.dma_start(x_in[:, :, :], x_v[0]).then_inc(x_loaded, 16)
            sp.dma_start(adj_in[:, :, :], adj_v[0]).then_inc(adj_loaded, 16)
            for dst, src in wide:
                sp.dma_start(dst, src).then_inc(weights_loaded, 16)

            def load(n):
                sp.wait_ge(xT0_psum, n)
                sp.wait_ge(xb_ready, n)
                sp.dma_start(x_in[:, :, :], graph(x_v, n)).then_inc(x_loaded, 16)
                sp.wait_ge(negm_ready, n)
                sp.wait_ge(adjb_ready, n)
                sp.dma_start(adj_in[:, :, :], graph(adj_v, n)).then_inc(adj_loaded, 16)

            def store(n):
                sp.wait_ge(out_ready, n + 1)
                sp.dma_start(graph(out_v, n), out_tok[:, :, :]).then_inc(out_stored, 16)

            load(1)
            load(2)
            store(0)
            with sp.Fori(2, G - 1) as i:
                load(i + 1)
                store(i - 1)
            store(G - 2)
            store(G - 1)
            sp.wait_ge(out_stored, 16 * G)

        @block.gpsimd
        def _(pool):
            nc.gpsimd.memset(kP0[:, :, :], 0.0).then_inc(kpad_zeroed, 1)
            nc.gpsimd.memset(kP1[:, :, :], 0.0).then_inc(kpad_zeroed, 1)
            nc.gpsimd.memset(minus_half[:, :], -0.5).then_inc(half_ready, 1)
            nc.gpsimd.memset(ident[:, :], 0.0).then_inc(zeroed, 1)
            pool.wait_ge(zeroed, 1)
            nc.gpsimd.affine_select(out=ident[:, :], in_=ident[:, :], compare_op=ALU.not_equal, fill=1.0,
                                    base=0, pattern=[[-1, P]], channel_multiplier=1).then_inc(ident_ready, 1)
            pool.wait_ge(half_ready, 1)
            pool.wait_ge(weights_loaded, 16 * len(wide))

            def vec(name):
                return rep[name][:, :, :].to_broadcast([P, T, D])

            def rstd(key, n):
                _, _, var, rs = ln[key]
                _, _, var_ready, rstd_ready = ln_sem[key]
                pool.wait_ge(var_ready, n + 1)
                nc.gpsimd.tensor_tensor(rs[:, :], var[:, :], minus_half[:, :], ALU.pow).then_inc(rstd_ready, 1)

            def x0(n):
                pool.wait_ge(x_loaded, 16 * (n + 1))
                if later(n):
                    pool.wait_ge(x1_ready, n)
                nc.gpsimd.tensor_tensor(xb[:, :, :], x_in[:, :, :], vec("L0_gnn_b2"), ALU.add).then_inc(xb_ready, 1)

            def O0_(n):
                rstd("a0", n)

            def F0(n):
                rstd("b0", n)

            def Y0(n):
                pool.wait_ge(y0_ready, n + 1)
                nc.gpsimd.tensor_tensor(y0g[:, :, :], y0[:, :, :], vec("L0_gnn_g2"), ALU.mult).then_inc(y0g_ready, 1)
                pool.wait_ge(y0g_ready, n + 1)
                pool.wait_ge(xb_ready, n + 1)
                if later(n):
                    pool.wait_ge(xT1_psum, n)
                nc.gpsimd.tensor_tensor(x1[:, :, :], y0g[:, :, :], xb[:, :, :], ALU.add).then_inc(x1_ready, 1)

            def x1_(n):
                pool.wait_ge(x1_ready, n + 1)
                if later(n):
                    pool.wait_ge(r1_ready, n)
                nc.gpsimd.tensor_tensor(x1b[:, :, :], x1[:, :, :], vec("L1_gnn_bo"), ALU.add).then_inc(x1b_ready, 1)

            def W1(n):
                rstd("a1", n)

            def X1(n):
                pool.wait_ge(n1_ready, n + 1)
                nc.gpsimd.tensor_tensor(n1g[:, :, :], n1[:, :, :], vec("L1_gnn_g1"), ALU.mult).then_inc(n1g_ready, 1)
                pool.wait_ge(n1g_ready, n + 1)
                nc.gpsimd.tensor_tensor(x2[:, :, :], n1g[:, :, :], vec("L1_gnn_beta1"), ALU.add).then_inc(x2_ready, 1)
                pool.wait_ge(x2_ready, n + 1)
                if later(n):
                    pool.wait_ge(r2_ready, n)
                nc.gpsimd.tensor_tensor(x2b[:, :, :], x2[:, :, :], vec("L1_gnn_b2"), ALU.add).then_inc(x2b_ready, 1)

            def F2(n):
                rstd("b1", n)

            def Y1(n):
                pool.wait_ge(n2_ready, n + 1)
                nc.gpsimd.tensor_tensor(n2[:, :, :], n2[:, :, :], vec("L1_gnn_g2"), ALU.mult).then_inc(n2g_ready, 1)
                pool.wait_ge(n2g_ready, n + 1)
                if later(n):
                    pool.wait_ge(out_stored, 16 * n)
                nc.gpsimd.tensor_tensor(out_tok[:, :, :], n2[:, :, :], vec("L1_gnn_beta2"), ALU.add).then_inc(out_ready, 1)

            all_graphs(pool, {"x0": x0, "O0": O0_, "F0": F0, "Y0": Y0, "x1": x1_, "W1": W1, "X1": X1,
                              "F2": F2, "Y1": Y1})

        @block.scalar
        def _(act):
            for dst, src in narrow:
                act.dma_start(dst, src, allow_slow_non_contiguous=True).then_inc(cols_loaded, 16)
            act.wait_ge(ident_ready, 1)
            nc.scalar.copy(identb[:, :], ident[:, :]).then_inc(identb_ready, 1)
            for o in range(2 * C):
                act.wait_ge(wfT_psum, o + 1)
                nc.scalar.copy(wf0[:, o, :], [S0, G0][o % 2][:, 0:D]).then_inc(wf_ready, 1)
            act.wait_ge(kpad_zeroed, 2)
            act.wait_ge(cols_loaded, 16 * len(narrow))
            nc.scalar.mul(bqs[:, :], col["L1_gnn_bq"][:, :], SCALE).then_inc(bqs_ready, 1)
            act.wait_ge(bqs_ready, 1)

            def x0(n):
                act.wait_ge(xT0_psum, n + 1)
                nc.scalar.copy(xT0[:, :, :], two(T0)).then_inc(xT0_ready, 1)

            def q0(n):
                act.wait_ge(q0_psum, n + 1)
                nc.scalar.copy(qT0[:, :, :], two(S0)).then_inc(q0_ready, 1)

            def k0(n):
                act.wait_ge(k0_psum, n + 1)
                for q in range(Q):
                    rows = slice(DH * q, DH * q + DH)
                    last = nc.scalar.copy(kP0[rows, q:H:Q, :], two(G0)[rows])
                last.then_inc(k0_ready, 1)

            def v0(n):
                act.wait_ge(v0_psum, n + 1)
                nc.scalar.copy(V0[:, :, :], two(O0)).then_inc(v0_ready, 1)

            def R0(n, u):
                act.wait_ge(scores0, n * U + u + 1)
                if u >= 2 or later(n):
                    act.wait_ge(pT0_psum, n * U + u - 1)
                nc.scalar.activation(P0[:, u % 2, :, :], two([S0, G0][u % 2]), ACT.Relu, scale=SLOPE - 1.0)\
                    .then_inc(relu0_ready, 1)

            def S0_(n, u):
                c, q, t = unit(u)
                act.wait_ge(leaky0_ready, n * U + u + 1)
                pb = P0[:, u % 2, :, :]
                for k in range(2):
                    h = Q * c + q + k
                    last = nc.scalar.activation(pb[:, k, :], pb[:, k, :], ACT.Exp, bias=nb0[:, u, k:k + 1],
                                                scale=-1.0, accum_out=sum0[:, t, h:h + 1])
                last.then_inc(exp0_ready, 1)

            def T0_(n, u):
                c, q, t = unit(u)
                act.wait_ge(pT0_psum, n * U + u + 1)
                nc.scalar.copy(PT0[:, c, q:q + 2, :, P * t:P * t + P],
                               T0[:, :].rearrange("p (k j i) -> p k j i", k=2, j=T)).then_inc(PT0_ready, 1)

            def O0_(n):
                act.wait_ge(av0_psum, n * C + C)
                nc.scalar.copy(oT0[:, :, :], two(O0)).then_inc(oT0_ready, 1)

            def N0(n):
                act.wait_ge(zT0_psum, n + 1)
                for c in range(C):
                    last = nc.scalar.activation(zf0[:, c, :], two(T0)[:, c, :], ACT.Identity,
                                                bias=col["L0_gnn_b1"][:, c:c + 1], scale=col["L0_gnn_g1"][:, c:c + 1])
                last.then_inc(zf0_ready, 1)

            def x1_(n):
                act.wait_ge(xT1_psum, n + 1)
                nc.scalar.copy(xT1[:, :, :], two(T1)).then_inc(xT1_ready, 1)

            def q1(n):
                act.wait_ge(q1_psum, n + 1)
                for c in range(C):
                    last = nc.scalar.activation(qT1[:, c, :], two(S1)[:, c, :], ACT.Identity,
                                                bias=bqs[:, c:c + 1], scale=SCALE)
                last.then_inc(q1_ready, 1)

            def k1(n):
                act.wait_ge(k1_psum, n + 1)
                for h in range(H):
                    c, rows = h // Q, slice(DH * (h % Q), DH * (h % Q) + DH)
                    last = nc.scalar.activation(kP1[rows, h, :], two(G1)[rows, c, :], ACT.Identity,
                                                bias=col["L1_gnn_bk"][rows, c:c + 1])
                last.then_inc(k1_ready, 1)

            def S1_(n, u):
                c, q, t = unit(u)
                act.wait_ge(bias1_ready, n * U + u + 1)
                if u >= 2 or later(n):
                    act.wait_ge(pT1_psum, n * U + u - 1)
                for k in range(2):
                    h = Q * c + q + k
                    last = nc.scalar.activation(P1[:, u % 2, k, :], two([S1, G1][u % 2])[:, k, :], ACT.Exp,
                                                bias=nb1[:, u, k:k + 1],
                                                accum_out=sum1[:, t, h:h + 1])
                last.then_inc(exp1_ready, 1)

            def W1(n):
                act.wait_ge(av1_psum, (n * C + C) * R)
                nc.scalar.copy(oT1[:, :, :], two(O1)).then_inc(oT1_ready, 1)

            def X1(n):
                act.wait_ge(x2T_psum, n + 1)
                nc.scalar.copy(x2T[:, :, :], two(T1)).then_inc(x2T_ready, 1)

            def F1(n, g):
                act.wait_ge(up_psum, n * FB + g + 1)
                for k in range(2):
                    f = 2 * g + k
                    last = nc.scalar.activation(gT[:, f, :], two([S1, G1, O1, T1][g])[:, k, :], ACT.Gelu,
                                                bias=col["L1_gnn_b1"][:, f:f + 1])
                last.then_inc(gT_ready, 1)

            all_graphs(act, {"x0": x0, "q0": q0, "k0": k0, "v0": v0, "R0": R0, "S0": S0_, "T0": T0_, "O0": O0_,
                             "N0": N0, "x1": x1_, "q1": q1, "k1": k1, "S1": S1_, "W1": W1, "X1": X1, "F1": F1})

        @block.vector
        def _(dve):
            dve.wait_ge(weights_loaded, 16 * len(wide))

            def stats(key, n, tile):
                st, mv, ve, _ = ln[key]
                stats_done, moments_done, var_ready, _ = ln_sem[key]
                for t in range(T):
                    last = nc.vector.bn_stats(st[:, t, :], tile[:, t, :])
                last.then_inc(stats_done, 1)
                dve.wait_ge(stats_done, n + 1)
                nc.vector.memset(held[:, :], 0.0)
                for t in range(T):
                    last = nc.vector.bn_aggr(mv[:, t, :], st[:, t, :])
                last.then_inc(moments_done, 1)
                dve.wait_ge(moments_done, n + 1)
                nc.vector.tensor_scalar_add(ve[:, :], mv[:, :, 1], EPS).then_inc(var_ready, 1)

            def normalise(key, n, dst, src, done):
                _, mv, _, rs = ln[key]
                dve.wait_ge(ln_sem[key][3], n + 1)
                for t in range(T):
                    last = nc.vector.tensor_scalar(dst[:, t, :], src[:, t, :], mv[:, t, 0:1], rs[:, t:t + 1],
                                                   ALU.subtract, ALU.mult)
                last.then_inc(done, 1)

            def x0(n):
                dve.wait_ge(adj_loaded, 16 * (n + 1))
                nc.vector.tensor_scalar(negm[:, :, :], adj_in[:, :, :], 0.0, NEG, ALU.is_le, ALU.mult)\
                    .then_inc(negm_ready, 1)

            def adj0(n):
                if later(n):
                    dve.wait_ge(adjT_psum, n)
                nc.vector.tensor_copy(adjb[:, :, :], adj_in[:, :, :]).then_inc(adjb_ready, 1)

            def S0_(n, u):
                dve.wait_ge(relu0_ready, n * U + u + 1)
                nc.vector.memset(held[:, :], 0.0)
                for k in range(2):
                    pb = P0[:, u % 2, k, :]
                    last = nc.vector.tensor_tensor_reduce(out=pb, in0=two([S0, G0][u % 2])[:, k, :], in1=pb,
                                                          scale=-1.0, scalar=BIG, op0=ALU.add, op1=ALU.min,
                                                          accum_out=nb0[:, u, k:k + 1])
                last.then_inc(leaky0_ready, 1)

            def O0_(n):
                dve.wait_ge(exp0_ready, n * U + U)
                nc.vector.reciprocal(rinv0[:, :, :], sum0[:, :, :]).then_inc(rinv0_ready, 1)
                dve.wait_ge(rinv0_ready, n + 1)
                dve.wait_ge(o0_psum, n + 1)
                nc.vector.tensor_tensor(h0[:, :, :].rearrange("p t (h d) -> p (t h) d", d=DH),
                                        S0[:, :].rearrange("p (a d) -> p a d", d=DH),
                                        rinv0[:, :, :].rearrange("p t (h o) -> p (t h) o", o=1).to_broadcast([P, T * H, DH]),
                                        ALU.mult).then_inc(h0_ready, 1)
                dve.wait_ge(h0_ready, n + 1)
                stats("a0", n, h0)

            def N0(n):
                normalise("a0", n, z0, h0, z0_ready)

            def F0(n):
                dve.wait_ge(ffn0_psum, n + 1)
                stats("b0", n, two(G0))

            def Y0(n):
                if later(n):
                    dve.wait_ge(y0g_ready, n)
                normalise("b0", n, y0, two(G0), y0_ready)

            def m1(n):
                dve.wait_ge(adjT_psum, n + 1)
                aT = O1[:, 0:N].bitcast(BF16).rearrange("p (j i) -> p j i", j=T)
                for r in range(R):
                    last = nc.vector.tensor_scalar(M1[:, r, :, :], aT, float(r), None, ALU.is_equal)
                last.then_inc(mask_ready, 1)

            def v1(n, r):
                dve.wait_ge(v1_psum, n * R + r + 1)
                nc.vector.tensor_tensor(V1[:, r, :, :], two([T1, O1][r % 2]), bv[:, r, :, :].to_broadcast([P, T, D]),
                                        ALU.add).then_inc(v1_ready, 1)

            def S1_(n, u):
                dve.wait_ge(scores1, n * U + u + 1)
                nc.vector.tensor_reduce(nb1[:, u, :], two([S1, G1][u % 2]), AX.X, ALU.max, negate=True)\
                    .then_inc(bias1_ready, 1)

            def T1_(n, u):
                c, q, t = unit(u)
                dve.wait_ge(pT1_psum, n * U + u + 1)
                if u == 0:
                    dve.wait_ge(mask_ready, n + 1)
                for r in range(R):
                    if u == 4:
                        dve.wait_ge(av1_psum, n * C * R + r + 1)
                    last = nc.vector.tensor_tensor(A1[:, r, q:q + 2, :, P * t:P * t + P],
                                                   T1[:, :].rearrange("p (k j i) -> p k j i", k=2, j=T),
                                                   M1[:, r:r + 1, :, P * t:P * t + P].to_broadcast([P, 2, T, P]),
                                                   ALU.mult)
                last.then_inc(A1_ready, 1)

            def W1(n):
                dve.wait_ge(exp1_ready, n * U + U)
                nc.vector.reciprocal(rinv1[:, :, 0], sum1[:, :, :].rearrange("p t h -> p (t h)")).then_inc(rinv1_ready, 1)
                dve.wait_ge(rinv1_ready, n + 1)
                nc.vector.tensor_copy(rsp1[:, :, :].rearrange("p t (h d) -> p (t h) d", d=DH),
                                      rinv1[:, :, :].to_broadcast([P, T * H, DH])).then_inc(rsp1_ready, 1)
                dve.wait_ge(oT1_ready, n + 1)
                dve.wait_ge(rT1_psum, n + 1)
                nc.vector.tensor_tensor(at1[:, :, :], two(S1), oT1[:, :, :], ALU.mult).then_inc(at1_ready, 1)
                dve.wait_ge(wo1_psum, n + 1)
                dve.wait_ge(x1b_ready, n + 1)
                nc.vector.tensor_tensor(r1[:, :, :], two(G1), x1b[:, :, :], ALU.add).then_inc(r1_ready, 1)
                dve.wait_ge(r1_ready, n + 1)
                stats("a1", n, r1)

            def X1(n):
                if later(n):
                    dve.wait_ge(n1g_ready, n)
                normalise("a1", n, n1, r1, n1_ready)

            def F2(n):
                dve.wait_ge(down_psum, n + 1)
                dve.wait_ge(x2b_ready, n + 1)
                nc.vector.tensor_tensor(r2[:, :, :], two(S1), x2b[:, :, :], ALU.add).then_inc(r2_ready, 1)
                dve.wait_ge(r2_ready, n + 1)
                stats("b1", n, r2)

            def Y1(n):
                if later(n):
                    dve.wait_ge(out_ready, n)
                normalise("b1", n, n2, r2, n2_ready)

            all_graphs(dve, {"x0": x0, "adj0": adj0, "S0": S0_, "O0": O0_, "N0": N0, "F0": F0, "Y0": Y0,
                             "m1": m1, "v1": v1, "S1": S1_, "T1": T1_, "W1": W1, "X1": X1, "F2": F2, "Y1": Y1})

        @block.tensor
        def _(pe):
            pe.wait_ge(ident_ready, 1)
            pe.wait_ge(weights_loaded, 16 * len(wide))
            for o in range(2 * C):
                if o >= 2:
                    pe.wait_ge(wf_ready, o - 1)
                for c in range(C):
                    last = nc.tensor.transpose([S0, G0][o % 2][:, P * c:P * c + P],
                                               wf0_in[:, c, P * o:P * o + P], ident[:, :])
                last.then_inc(wfT_psum, 1)
            pe.wait_ge(wf_ready, 2 * C)
            pe.wait_ge(identb_ready, 1)

            def mm(out_, lhsT, rhs, start, stop):
                return nc.tensor.matmul(out_, lhsT, rhs, start=start, stop=stop)

            def flip(bank_, tile):
                for a in range(2):
                    for b in range(2):
                        last = nc.tensor.transpose(two(bank_)[:, a, P * b:P * b + P],
                                                   tile[:, b, P * a:P * a + P], ident[:, :])
                return last

            def channels(bank_, weight, xT, cols=0):
                for o in range(2):
                    for c in range(C):
                        last = mm(two(bank_)[:, o, :], weight[:, c, cols + P * o:cols + P * o + P], xT[:, c, :],
                                  c == 0, c == C - 1)
                return last

            def nodes(bank_, pairs):
                for t in range(T):
                    for k, (xT, weight) in enumerate(pairs):
                        last = mm(two(bank_)[:, t, :], xT[:, P * t:P * t + P], weight, k == 0, k == len(pairs) - 1)
                return last

            def x0(n):
                pe.wait_ge(x_loaded, 16 * (n + 1))
                if later(n):
                    pe.wait_ge(zf0_ready, n)
                flip(T0, x_in).then_inc(xT0_psum, 1)

            def q0(n):
                pe.wait_ge(xT0_ready, n + 1)
                if later(n):
                    pe.wait_ge(h0_ready, n)
                channels(S0, wq0, xT0).then_inc(q0_psum, 1)

            def k0(n):
                if later(n):
                    pe.wait_ge(y0_ready, n)
                channels(G0, wk0, xT0).then_inc(k0_psum, 1)

            def v0(n):
                if later(n):
                    pe.wait_ge(oT0_ready, n)
                nodes(O0, [(xT0[:, c, :], wv0[:, c, :]) for c in range(C)]).then_inc(v0_psum, 1)

            def R0(n, u):
                c, q, t = unit(u)
                if u == 0:
                    pe.wait_ge(q0_ready, n + 1)
                    pe.wait_ge(k0_ready, n + 1)
                    pe.wait_ge(negm_ready, n + 1)
                if u >= 2:
                    pe.wait_ge(leaky0_ready, n * U + u - 1)
                b = [S0, G0][u % 2]
                mm(two(b), identb[:, :], negm[:, t:t + 1, :].to_broadcast([P, 2, N]), True, False)
                for k in range(2):
                    last = mm(two(b)[:, k, :], qT0[:, c, P * t:P * t + P], kP0[:, Q * c + q + k, :], False, k == 1)
                last.then_inc(scores0, 1)

            def blocks(bank_, probs):
                for k in range(2):
                    for j in range(T):
                        at = P * (T * k + j)
                        last = nc.tensor.transpose(bank_[:, at:at + P], probs[:, k, P * j:P * j + P], ident[:, :])
                return last

            def T0_(n, u):
                pe.wait_ge(exp0_ready, n * U + u + 1)
                if u:
                    pe.wait_ge(PT0_ready, n * U + u)
                blocks(T0, P0[:, u % 2, :, :]).then_inc(pT0_psum, 1)

            def A0(n, c):
                pe.wait_ge(PT0_ready, n * U + 4 * c + 4)
                if c == 0:
                    pe.wait_ge(v0_ready, n + 1)
                for j in range(T):
                    for q in range(Q):
                        h = Q * c + q
                        last = mm(two(O0)[DH * q:DH * q + DH, c, :], V0[:, j, DH * h:DH * h + DH],
                                  PT0[:, c, q, j, :], j == 0, j == T - 1)
                last.then_inc(av0_psum, 1)

            def O0_(n):
                pe.wait_ge(oT0_ready, n + 1)
                pe.wait_ge(leaky0_ready, n * U + U - 1)
                flip(S0, oT0).then_inc(o0_psum, 1)

            def N0(n):
                pe.wait_ge(z0_ready, n + 1)
                pe.wait_ge(PT0_ready, n * U + U)
                flip(T0, z0).then_inc(zT0_psum, 1)

            def F0(n):
                pe.wait_ge(zf0_ready, n + 1)
                pe.wait_ge(leaky0_ready, n * U + U)
                nodes(G0, [(zf0[:, c, :], wf0[:, c, :]) for c in range(C)] +
                      [(xT0[:, c, :], wf0[:, C + c, :]) for c in range(C)]).then_inc(ffn0_psum, 1)

            def x1_(n):
                pe.wait_ge(x1_ready, n + 1)
                if later(n):
                    pe.wait_ge(gT_ready, n * FB)
                flip(T1, x1).then_inc(xT1_psum, 1)

            def m1(n):
                pe.wait_ge(adjb_ready, n + 1)
                if later(n):
                    pe.wait_ge(gT_ready, n * FB - 1)
                ob = O1[:, 0:N].bitcast(BF16)
                for j in range(T):
                    for t in range(T):
                        at = N * j + P * t
                        last = nc.tensor.transpose(ob[:, at:at + P], adjb[:, t, P * j:P * j + P], identb[:, :])
                last.then_inc(adjT_psum, 1)

            def q1(n):
                pe.wait_ge(xT1_ready, n + 1)
                if later(n):
                    pe.wait_ge(r2_ready, n)
                channels(S1, wq1, xT1).then_inc(q1_psum, 1)

            def k1(n):
                if later(n):
                    pe.wait_ge(gT_ready, n * FB - 2)
                channels(G1, wk1, xT1).then_inc(k1_psum, 1)

            def v1(n, r):
                if r == 0:
                    pe.wait_ge(xT1_ready, n + 1)
                elif r == 1:
                    pe.wait_ge(mask_ready, n + 1)
                else:
                    pe.wait_ge(v1_ready, n * R + r - 1)
                nodes([T1, O1][r % 2], [(xT1[:, c, :], wv1[:, r, c, :]) for c in range(C)]).then_inc(v1_psum, 1)

            def S1_(n, u):
                c, q, t = unit(u)
                if u == 0:
                    pe.wait_ge(q1_ready, n + 1)
                    pe.wait_ge(k1_ready, n + 1)
                if u >= 2:
                    pe.wait_ge(exp1_ready, n * U + u - 1)
                for k in range(2):
                    last = mm(two([S1, G1][u % 2])[:, k, :], qT1[:, c, P * t:P * t + P], kP1[:, Q * c + q + k, :],
                              True, True)
                last.then_inc(scores1, 1)

            def T1_(n, u):
                pe.wait_ge(exp1_ready, n * U + u + 1)
                if u:
                    pe.wait_ge(A1_ready, n * U + u)
                else:
                    pe.wait_ge(v1_ready, n * R + R - 1)
                blocks(T1, P1[:, u % 2, :, :]).then_inc(pT1_psum, 1)

            def A1_(n, c):
                pe.wait_ge(A1_ready, n * U + 4 * c + 4)
                if c == 0:
                    pe.wait_ge(v1_ready, n * R + R)
                for r in range(R):
                    for j in range(T):
                        for q in range(Q):
                            h = Q * c + q
                            last = mm(two(O1)[DH * q:DH * q + DH, c, :], V1[:, r, j, DH * h:DH * h + DH],
                                      A1[:, r, q, j, :], r == 0 and j == 0, r == R - 1 and j == T - 1)
                    last.then_inc(av1_psum, 1)

            def W1(n):
                pe.wait_ge(rsp1_ready, n + 1)
                pe.wait_ge(exp1_ready, n * U + U - 1)
                flip(S1, rsp1).then_inc(rT1_psum, 1)
                pe.wait_ge(at1_ready, n + 1)
                pe.wait_ge(exp1_ready, n * U + U)
                nodes(G1, [(at1[:, c, :], wo1[:, c, :]) for c in range(C)]).then_inc(wo1_psum, 1)

            def X1(n):
                pe.wait_ge(x2_ready, n + 1)
                pe.wait_ge(A1_ready, n * U + U)
                flip(T1, x2).then_inc(x2T_psum, 1)

            def F1(n, g):
                if g == 0:
                    pe.wait_ge(at1_ready, n + 1)
                    pe.wait_ge(x2T_ready, n + 1)
                elif g == 1:
                    pe.wait_ge(r1_ready, n + 1)
                elif g == 2:
                    pe.wait_ge(oT1_ready, n + 1)
                channels([S1, G1, O1, T1][g], w1, x2T, cols=2 * P * g).then_inc(up_psum, 1)

            def F2(n):
                pe.wait_ge(gT_ready, n * FB + FB)
                nodes(S1, [(gT[:, f, :], w2[:, f, :]) for f in range(FC)]).then_inc(down_psum, 1)

            all_graphs(pe, {"x0": x0, "q0": q0, "k0": k0, "v0": v0, "R0": R0, "T0": T0_, "A0": A0, "O0": O0_,
                            "N0": N0, "F0": F0, "x1": x1_, "m1": m1, "q1": q1, "k1": k1, "v1": v1, "S1": S1_,
                            "T1": T1_, "A1": A1_, "W1": W1, "X1": X1, "F1": F1, "F2": F2})


WEIGHTS = ["L0_gnn_Wq", "L0_gnn_Wk", "L0_gnn_Wv", "L0_gnn_Wffn", "L0_gnn_g1", "L0_gnn_b1", "L0_gnn_g2",
           "L0_gnn_b2", "L1_gnn_Wq", "L1_gnn_bq", "L1_gnn_Wk", "L1_gnn_bk", "L1_gnn_Wv", "L1_gnn_bv",
           "L1_gnn_Wo", "L1_gnn_bo", "L1_gnn_W1", "L1_gnn_b1", "L1_gnn_W2", "L1_gnn_b2", "L1_gnn_g1",
           "L1_gnn_beta1", "L1_gnn_g2", "L1_gnn_beta2"]


def kernel(**inputs):
    import numpy as _np
    import concourse.bacc as _bacc
    from concourse import mybir as _mybir
    from concourse.bass_utils import run_bass_kernel_spmd as _run

    nc = _bacc.Bacc("TRN2", target_bir_lowering=False, num_devices=1)
    arrays, aps = {}, {}
    for name in ["x", "adj"] + WEIGHTS:
        a = _np.ascontiguousarray(inputs[name])
        arrays[f"in_{name}"] = a
        aps[name] = nc.dram_tensor(f"in_{name}", a.shape, _mybir.dt.from_np(a.dtype), kind="ExternalInput").ap()
    out = nc.dram_tensor("out_x", arrays["in_x"].shape, _mybir.dt.float32, kind="ExternalOutput").ap()
    graph_layers_kernel(nc, aps["x"], aps["adj"], {name: aps[name] for name in WEIGHTS}, out)
    r = _run(nc, [arrays], core_ids=[0])
    return r.results[0]["out_x"]
```

```python
from contextlib import ExitStack

import concourse.bass as bass
from concourse import mybir

F32 = mybir.dt.float32
F32R = mybir.dt.float32r
BF16 = mybir.dt.bfloat16
I32 = mybir.dt.int32
ALU = mybir.AluOpType
ACT = mybir.ActivationFunctionType
AX = mybir.AxisListType

P = 128
D = 256
N = 256
C = D // P
T = N // P
H, DH = 8, 32
Q = P // DH
STACKS = 3 * Q * 16
ST = 3 * DH
R = 4
FF = 1024
FC = FF // P
FB = FC // 2
U = H * T // 2
NEG = -float(2 ** 53)
SLOPE = 0.2
EPS = 1e-5
BIG = 3e38
SCALE = float(DH) ** -0.5


def unit(u):
    return u // 4, 2 * (u % 4 // 2), u % 2


def last_graph(n, G):
    return isinstance(n, int) and n == G - 1


def later(n):
    return not (isinstance(n, int) and n == 0)


ORDER_TEXT = """
x0/1 load_x/0 S1.7/3 v0/1 T1.6/3 q0/1 T1.7/3 k0/1 x1/2 q1/2 k1/2 A1.1/3 V1/3 m0/1 W1/3 m1/2 v1.0/2
R0.0/1 S0.0/1 v1.1/2 b1/2 R0.1/1 r1/3 v1.2/2 T0.0/1 R0.2/1 X1/3 v1.3/2 F1.0/3 S0.1/1 F1.1/3 F1.2/3
F1.3/3 R0.3/1 T0.1/1 S0.2/1 F2/3 S0.3/1 T0.2/1 R0.4/1 T0.3/1 r2/3 Y1/3 S1.0/2 R0.5/1 S0.4/1 S1.1/2
A0.0/1 S0.5/1 T1.0/2 R0.6/1 T0.4/1 S1.2/2 S0.6/1 T1.1/2 T0.5/1 R0.7/1 T0.6/1 S0.7/1 S1.3/2 T1.2/2 T0.7/1
S1.4/2 S1.5/2 adj0/1 load_adj/0 T1.3/2 A0.1/1 o0/1 O0/1 A1.0/2 N0/1 S1.6/2 T1.4/2 F0/1 T1.5/2 Y0/1
"""
ORDER = [(name.split(".")[0], *map(int, name.split(".")[1:]), int(lag))
         for name, lag in (entry.split("/") for entry in ORDER_TEXT.split())]
LAG = max(s[-1] for s in ORDER)


def graph_layers_kernel(nc, x, adj, w, out):
    G = x.shape[0]
    ctx = ExitStack()
    with ctx:
        def sb(name, shape, dt=F32):
            return ctx.enter_context(nc.sbuf_tensor(name, shape, dt))

        def bank(name):
            return ctx.enter_context(nc.psum_tensor(name, [P, 512], F32))

        def sem(name):
            return ctx.enter_context(nc.semaphore(name))

        ident = sb("ident", [P, P])
        identb = sb("identb", [P, P], BF16)
        wq0, wk0, wv0 = (sb(f"w{a}0_sb", [P, C, D]) for a in "qkv")
        wf0 = sb("wf0", [P, 2 * C, D])
        wq1, wk1, wo1 = (sb(f"w{a}1_sb", [P, C, D]) for a in "qko")
        wv1 = sb("wv1_sb", [P, R, C, D])
        w1 = sb("w1_sb", [P, C, FF])
        w2 = sb("w2_sb", [P, FC, D])
        rep = {name: sb(f"rep_{name}", [P, 1, D]) for name in
               ("L0_gnn_g2", "L0_gnn_b2", "L1_gnn_bo", "L1_gnn_g1", "L1_gnn_beta1", "L1_gnn_b2",
                "L1_gnn_g2", "L1_gnn_beta2")}
        bv = sb("bv_rep", [P, R, 1, D])
        col = {name: sb(f"col_{name}", [P, n]) for name, n in
               (("L0_gnn_g1", C), ("L0_gnn_b1", C), ("L1_gnn_bq", C), ("L1_gnn_bk", C), ("L1_gnn_b1", FC),
                ("L1_gnn_g1", C), ("L1_gnn_beta1", C))}
        minus_half = sb("minus_half", [P, T])
        held = sb("held", [P, U + 4])
        bqs = sb("bqs", [P, C])

        x_in = sb("x_in", [P, T, D])
        adj_in = sb("adj_in", [P, T, N], I32)
        xb = sb("xb", [P, T, D])
        negm = sb("negm", [P, T, N], BF16)
        adjb = sb("adjb", [P, T, N], BF16)
        xT0 = sb("xT0", [P, C, N])
        qh0, ql0, kh0, kl0 = (sb(a, [P, C, N], F32R) for a in ("qh0", "ql0", "kh0", "kl0"))
        Qs0, Ks0 = (sb(a, [ST, Q, C, N], F32R) for a in ("Qs0", "Ks0"))
        V0 = sb("V0", [P, T, D])
        P0 = sb("P0", [P, 2, 2, N])
        PT0 = sb("PT0", [P, Q, T, N])
        nb0 = sb("nb0", [P, U, 2])
        sum0 = sb("sum0", [P, T, H])
        rinv0 = sb("rinv0", [P, T, H])
        oT0 = sb("oT0", [P, C, N])
        h0 = sb("h0", [P, T, D])
        zf0 = sb("zf0", [P, C, N])
        y0 = sb("y0", [P, T, D])
        x1 = sb("x1", [P, T, D])
        x1b = sb("x1b", [P, T, D])
        xT1 = sb("xT1", [P, C, N])
        M1 = sb("M1", [P, R, T, N], BF16)
        qh1, ql1, kh1, kl1 = (sb(a, [P, C, N], F32R) for a in ("qh1", "ql1", "kh1", "kl1"))
        Qs1, Ks1 = (sb(a, [ST, Q, C, N], F32R) for a in ("Qs1", "Ks1"))
        V1 = sb("V1", [P, R, T, D])
        P1 = sb("P1", [P, 2, 2, N])
        A1 = sb("A1", [P, R, Q, T, N])
        nb1 = sb("nb1", [P, U, 2])
        sum1 = sb("sum1", [P, T, H])
        rinv1 = sb("rinv1", [P, T * H, 1])
        rsp1 = sb("rsp1", [P, T, D])
        r1 = sb("r1", [P, T, D])
        x2b = sb("x2b", [P, T, D])
        late = A1[:, :, :, :, :].rearrange("p r q t n -> p (r q t) n")
        gT, oT1, at1, x2T = late[:, 0:FC, :], late[:, FC:FC + C, :], late[:, FC + C:FC + 2 * C, :], \
            late[:, FC + 2 * C:FC + 3 * C, :]
        wf0_in = gT[:, 0:4, :].rearrange("p (c a) n -> p c (a n)", c=C)
        r2 = sb("r2", [P, T, D])
        out_tok = sb("out_tok", [P, T, D])
        ln = {k: (sb(f"st_{k}", [P, T, 6]), sb(f"mv_{k}", [P, T, 2]), sb(f"ve_{k}", [P, T]),
                  sb(f"rs_{k}", [P, T])) for k in ("a0", "b0", "a1", "b1")}
        ln_sem = {k: (sem(f"stats_{k}"), sem(f"moments_{k}"), sem(f"var_{k}_ready"), sem(f"rstd_{k}_ready"))
                  for k in ln}

        S0, G0, T0, O0 = bank("S0"), bank("G0"), bank("T0"), bank("O0")
        S1, G1, T1, O1 = bank("S1"), bank("G1"), bank("T1"), bank("O1")

        def two(b):
            return b[:, :].rearrange("p (a n) -> p a n", a=2)

        weights_loaded = sem("weights_loaded")
        cols_loaded = sem("cols_loaded")
        zeroed = sem("zeroed")
        ident_ready = sem("ident_ready")
        identb_ready = sem("identb_ready")
        half_ready = sem("half_ready")
        bqs_ready = sem("bqs_ready")
        wfT_psum = sem("wfT_psum")
        wf_ready = sem("wf_ready")
        x_loaded, adj_loaded, out_stored = sem("x_loaded"), sem("adj_loaded"), sem("out_stored")
        xT0_psum, xT0_ready, xb_ready = sem("xT0_psum"), sem("xT0_ready"), sem("xb_ready")
        negm_ready, adjb_ready = sem("negm_ready"), sem("adjb_ready")
        q0_psum, q0_ready, k0_psum, k0_ready = sem("q0_psum"), sem("q0_ready"), sem("k0_psum"), sem("k0_ready")
        qh0_ready, kh0_ready, qh1_ready, kh1_ready = (sem(a + "_ready") for a in ("qh0", "kh0", "qh1", "kh1"))
        q0_stacked, k0_stacked, q1_stacked, k1_stacked = (sem(a + "_stacked") for a in ("q0", "k0", "q1", "k1"))
        v0_psum, v0_ready = sem("v0_psum"), sem("v0_ready")
        scores0, relu0_ready = sem("scores0"), sem("relu0_ready")
        leaky0_ready, exp0_ready = sem("leaky0_ready"), sem("exp0_ready")
        pT0_psum, PT0_ready, av0_psum = sem("pT0_psum"), sem("PT0_ready"), sem("av0_psum")
        oT0_ready, o0_psum, rinv0_ready, h0_ready = sem("oT0_ready"), sem("o0_psum"), sem("rinv0_ready"), sem("h0_ready")
        z0_ready, zT0_psum, zf0_ready = sem("z0_ready"), sem("zT0_psum"), sem("zf0_ready")
        ffn0_psum, y0_ready, y0g_ready, x1_ready = sem("ffn0_psum"), sem("y0_ready"), sem("y0g_ready"), sem("x1_ready")
        xT1_psum, xT1_ready, x1b_ready = sem("xT1_psum"), sem("xT1_ready"), sem("x1b_ready")
        adjT_psum, mask_ready = sem("adjT_psum"), sem("mask_ready")
        q1_psum, q1_ready, k1_psum, k1_ready = sem("q1_psum"), sem("q1_ready"), sem("k1_psum"), sem("k1_ready")
        v1_psum, v1_ready = sem("v1_psum"), sem("v1_ready")
        scores1, bias1_ready, exp1_ready = sem("scores1"), sem("bias1_ready"), sem("exp1_ready")
        pT1_psum, A1_ready, av1_psum = sem("pT1_psum"), sem("A1_ready"), sem("av1_psum")
        oT1_ready, rinv1_ready, rsp1_ready, rT1_psum, at1_ready = sem("oT1_ready"), sem("rinv1_ready"), sem("rsp1_ready"), sem("rT1_psum"), sem("at1_ready")
        wo1_psum, r1_ready, n1_ready, n1g_ready = sem("wo1_psum"), sem("r1_ready"), sem("n1_ready"), sem("n1g_ready")
        x2b_ready, x2T_psum, x2T_ready = sem("x2b_ready"), sem("x2T_psum"), sem("x2T_ready")
        up_psum, gT_ready = sem("up_psum"), sem("gT_ready")
        down_psum, r2_ready, n2_ready, n2g_ready, out_ready = sem("down_psum"), sem("r2_ready"), sem("n2_ready"), sem("n2g_ready"), sem("out_ready")

        def chunks(a):
            return a.rearrange("(c p) o -> p c o", p=P)

        wide = [(wq0[:, :, :], chunks(w["L0_gnn_Wq"])), (wk0[:, :, :], chunks(w["L0_gnn_Wk"])),
                (wv0[:, :, :], chunks(w["L0_gnn_Wv"])), (wf0_in[:, :, :], chunks(w["L0_gnn_Wffn"])),
                (wq1[:, :, :], chunks(w["L1_gnn_Wq"])), (wk1[:, :, :], chunks(w["L1_gnn_Wk"])),
                (wo1[:, :, :], chunks(w["L1_gnn_Wo"])), (w1[:, :, :], chunks(w["L1_gnn_W1"])),
                (w2[:, :, :], chunks(w["L1_gnn_W2"]))]
        wide += [(wv1[:, r, :, :], chunks(w["L1_gnn_Wv"][r])) for r in range(R)]
        wide += [(rep[name][:, 0, :], w[name].partition_broadcast(P)) for name in rep]
        wide += [(bv[:, r, 0, :], w["L1_gnn_bv"][r].partition_broadcast(P)) for r in range(R)]
        narrow = [(col[name][:, :], w[name].rearrange("(c p) -> p c", p=P)) for name in col]
        x_v = x.rearrange("g (t p) d -> g p t d", p=P)
        adj_v = adj.rearrange("g (t p) m -> g p t m", p=P)
        out_v = out.rearrange("g (t p) d -> g p t d", p=P)

        def graph(view, n):
            if isinstance(n, int):
                return view[n]
            return view[bass.ds(n, 1)].rearrange("g p t d -> (g p) t d")

        def run_stages(stages, i):
            for name, *k, lag in ORDER:
                if name in stages and not (isinstance(i, int) and not 0 <= i - lag < G):
                    stages[name](i - lag, *k)

        def all_graphs(stages, fori):
            for i in range(LAG + 1):
                run_stages(stages, i)
            with fori(LAG + 1, G) as i:
                run_stages(stages, i)
            for i in range(G, G + LAG):
                run_stages(stages, i)

        block = ctx.enter_context(nc.Block())

        @block.sync
        def _(sp):
            for dst, src in wide:
                sp.dma_start(dst, src).then_inc(weights_loaded, 16)

            def load_x(n):
                if later(n):
                    sp.wait_ge(xT0_psum, n)
                    sp.wait_ge(xb_ready, n)
                sp.dma_start(x_in[:, :, :], graph(x_v, n)).then_inc(x_loaded, 16)

            def load_adj(n):
                if later(n):
                    sp.wait_ge(negm_ready, n)
                    sp.wait_ge(adjb_ready, n)
                sp.dma_start(adj_in[:, :, :], graph(adj_v, n)).then_inc(adj_loaded, 16)

            def stack(parts, dst, done):
                for b, part in enumerate(parts):
                    for q in range(Q):
                        sp.dma_start(dst[DH * b:DH * b + DH, q, :, :].bitcast(F32),
                                     part[DH * q:DH * q + DH, :, :].bitcast(F32)).then_inc(done, 16)

            def q0(n):
                sp.wait_ge(q0_ready, n + 1)
                stack((qh0, ql0, qh0), Qs0, q0_stacked)

            def k0(n):
                sp.wait_ge(k0_ready, n + 1)
                stack((kh0, kh0, kl0), Ks0, k0_stacked)

            def q1(n):
                sp.wait_ge(q1_ready, n + 1)
                stack((qh1, ql1, qh1), Qs1, q1_stacked)

            def k1(n):
                sp.wait_ge(k1_ready, n + 1)
                stack((kh1, kh1, kl1), Ks1, k1_stacked)

            def Y1(n):
                sp.wait_ge(out_ready, n + 1)
                sp.dma_start(graph(out_v, n), out_tok[:, :, :]).then_inc(out_stored, 16)

            all_graphs({"load_x": load_x, "load_adj": load_adj, "q0": q0, "k0": k0, "q1": q1, "k1": k1, "Y1": Y1},
                       sp.Fori)
            sp.wait_ge(out_stored, 16 * G)

        @block.gpsimd
        def _(pool):
            nc.gpsimd.memset(minus_half[:, :], -0.5).then_inc(half_ready, 1)
            nc.gpsimd.memset(ident[:, :], 0.0).then_inc(zeroed, 1)
            pool.wait_ge(zeroed, 1)
            nc.gpsimd.affine_select(out=ident[:, :], in_=ident[:, :], compare_op=ALU.not_equal, fill=1.0,
                                    base=0, pattern=[[-1, P]], channel_multiplier=1).then_inc(ident_ready, 1)
            pool.wait_ge(half_ready, 1)
            pool.wait_ge(weights_loaded, 16 * len(wide))

            nc.gpsimd.tensor_tensor(rep["L1_gnn_beta1"][:, :, :], rep["L1_gnn_beta1"][:, :, :],
                                    rep["L1_gnn_b2"][:, :, :], ALU.add).then_inc(zeroed, 1)
            pool.wait_ge(zeroed, 2)

            def vec(name):
                return rep[name][:, :, :].to_broadcast([P, T, D])

            def rstd(key, n):
                _, _, var, rs = ln[key]
                _, _, var_ready, rstd_ready = ln_sem[key]
                pool.wait_ge(var_ready, n + 1)
                nc.gpsimd.tensor_tensor(rs[:, :], var[:, :], minus_half[:, :], ALU.pow).then_inc(rstd_ready, 1)

            def x0(n):
                pool.wait_ge(x_loaded, 16 * (n + 1))
                if later(n):
                    pool.wait_ge(x1_ready, n)
                nc.gpsimd.tensor_tensor(xb[:, :, :], x_in[:, :, :], vec("L0_gnn_b2"), ALU.add).then_inc(xb_ready, 1)

            def O0_(n):
                rstd("a0", n)

            def F0(n):
                rstd("b0", n)

            def Y0(n):
                pool.wait_ge(y0_ready, n + 1)
                nc.gpsimd.tensor_tensor(y0[:, :, :], y0[:, :, :], vec("L0_gnn_g2"), ALU.mult).then_inc(y0g_ready, 1)
                pool.wait_ge(y0g_ready, n + 1)
                pool.wait_ge(xb_ready, n + 1)
                if later(n):
                    pool.wait_ge(xT1_psum, n)
                nc.gpsimd.tensor_tensor(x1[:, :, :], y0[:, :, :], xb[:, :, :], ALU.add).then_inc(x1_ready, 1)

            def b1(n):
                pool.wait_ge(x1_ready, n + 1)
                if later(n):
                    pool.wait_ge(r1_ready, n)
                nc.gpsimd.tensor_tensor(x1b[:, :, :], x1[:, :, :], vec("L1_gnn_bo"), ALU.add).then_inc(x1b_ready, 1)

            def r1_(n):
                rstd("a1", n)

            def X1(n):
                pool.wait_ge(n1_ready, n + 1)
                if later(n):
                    pool.wait_ge(r2_ready, n)
                nc.gpsimd.tensor_tensor(x2b[:, :, :], r1[:, :, :], vec("L1_gnn_g1"), ALU.mult).then_inc(n1g_ready, 1)
                pool.wait_ge(n1g_ready, n + 1)
                nc.gpsimd.tensor_tensor(x2b[:, :, :], x2b[:, :, :], vec("L1_gnn_beta1"), ALU.add).then_inc(x2b_ready, 1)

            def r2_(n):
                rstd("b1", n)

            def Y1(n):
                pool.wait_ge(n2_ready, n + 1)
                nc.gpsimd.tensor_tensor(r2[:, :, :], r2[:, :, :], vec("L1_gnn_g2"), ALU.mult).then_inc(n2g_ready, 1)
                pool.wait_ge(n2g_ready, n + 1)
                if later(n):
                    pool.wait_ge(out_stored, 16 * n)
                nc.gpsimd.tensor_tensor(out_tok[:, :, :], r2[:, :, :], vec("L1_gnn_beta2"), ALU.add).then_inc(out_ready, 1)

            all_graphs({"x0": x0, "O0": O0_, "F0": F0, "Y0": Y0, "b1": b1, "r1": r1_, "X1": X1,
                        "r2": r2_, "Y1": Y1}, pool.Fori)

        @block.scalar
        def _(act):
            for dst, src in narrow:
                act.dma_start(dst, src, allow_slow_non_contiguous=True).then_inc(cols_loaded, 16)
            act.wait_ge(ident_ready, 1)
            nc.scalar.copy(identb[:, :], ident[:, :]).then_inc(identb_ready, 1)
            for o in range(2 * C):
                act.wait_ge(wfT_psum, o + 1)
                nc.scalar.copy(wf0[:, o, :], [S0, G0][o % 2][:, 0:D]).then_inc(wf_ready, 1)
            act.wait_ge(cols_loaded, 16 * len(narrow))
            nc.scalar.mul(bqs[:, :], col["L1_gnn_bq"][:, :], SCALE).then_inc(bqs_ready, 1)
            act.wait_ge(weights_loaded, 16 * len(wide))
            nc.scalar.mul(wq1[:, :, :], wq1[:, :, :], SCALE).then_inc(bqs_ready, 1)
            act.wait_ge(bqs_ready, 2)

            def x0(n):
                act.wait_ge(xT0_psum, n + 1)
                nc.scalar.copy(xT0[:, :, :], two(T0)).then_inc(xT0_ready, 1)

            def q0(n):
                act.wait_ge(q0_psum, n + 1)
                nc.scalar.copy(qh0[:, :, :], two(S0)).then_inc(qh0_ready, 1)

            def k0(n):
                act.wait_ge(k0_psum, n + 1)
                nc.scalar.copy(kh0[:, :, :], two(G0)).then_inc(kh0_ready, 1)

            def v0(n):
                act.wait_ge(v0_psum, n + 1)
                nc.scalar.copy(V0[:, :, :], two(O0)).then_inc(v0_ready, 1)

            def R0(n, u):
                act.wait_ge(scores0, n * U + u + 1)
                if u >= 2 or later(n):
                    act.wait_ge(pT0_psum, n * U + u - 1)
                nc.scalar.activation(P0[:, u % 2, :, :], two([S0, G0][u % 2]), ACT.Relu, scale=SLOPE - 1.0)\
                    .then_inc(relu0_ready, 1)

            def S0_(n, u):
                c, q, t = unit(u)
                act.wait_ge(leaky0_ready, n * U + u + 1)
                pb = P0[:, u % 2, :, :]
                for k in range(2):
                    h = Q * c + q + k
                    last = nc.scalar.activation(pb[:, k, :], pb[:, k, :], ACT.Exp, bias=nb0[:, u, k:k + 1],
                                                scale=-1.0, accum_out=sum0[:, t, h:h + 1])
                last.then_inc(exp0_ready, 1)

            def T0_(n, u):
                c, q, t = unit(u)
                act.wait_ge(pT0_psum, n * U + u + 1)
                if u == 4:
                    act.wait_ge(av0_psum, n * C + 1)
                nc.scalar.copy(PT0[:, q:q + 2, :, P * t:P * t + P],
                               T0[:, :].rearrange("p (k j i) -> p k j i", k=2, j=T)).then_inc(PT0_ready, 1)

            def o0(n):
                act.wait_ge(av0_psum, n * C + C)
                nc.scalar.copy(oT0[:, :, :], two(O0)).then_inc(oT0_ready, 1)

            def N0(n):
                act.wait_ge(zT0_psum, n + 1)
                for c in range(C):
                    last = nc.scalar.activation(zf0[:, c, :], two(T0)[:, c, :], ACT.Identity,
                                                bias=col["L0_gnn_b1"][:, c:c + 1], scale=col["L0_gnn_g1"][:, c:c + 1])
                last.then_inc(zf0_ready, 1)

            def x1_(n):
                act.wait_ge(xT1_psum, n + 1)
                nc.scalar.copy(xT1[:, :, :], two(T1)).then_inc(xT1_ready, 1)

            def q1(n):
                act.wait_ge(q1_psum, n + 1)
                for c in range(C):
                    last = nc.scalar.activation(qh1[:, c, :], two(S1)[:, c, :], ACT.Identity, bias=bqs[:, c:c + 1])
                last.then_inc(qh1_ready, 1)

            def k1(n):
                act.wait_ge(k1_psum, n + 1)
                for c in range(C):
                    last = nc.scalar.activation(kh1[:, c, :], two(G1)[:, c, :], ACT.Identity,
                                                bias=col["L1_gnn_bk"][:, c:c + 1])
                last.then_inc(kh1_ready, 1)

            def S1_(n, u):
                c, q, t = unit(u)
                act.wait_ge(bias1_ready, n * U + u + 1)
                if u >= 2 or later(n):
                    act.wait_ge(pT1_psum, n * U + u - 1)
                for k in range(2):
                    h = Q * c + q + k
                    last = nc.scalar.activation(P1[:, u % 2, k, :], two([S1, G1][u % 2])[:, k, :], ACT.Exp,
                                                bias=nb1[:, u, k:k + 1],
                                                accum_out=sum1[:, t, h:h + 1])
                last.then_inc(exp1_ready, 1)

            def V1_(n):
                act.wait_ge(av1_psum, (n * C + C) * R)
                nc.scalar.copy(oT1[:, :, :], two(O1)).then_inc(oT1_ready, 1)

            def X1(n):
                act.wait_ge(x2T_psum, n + 1)
                for c in range(C):
                    last = nc.scalar.activation(x2T[:, c, :], two(T1)[:, c, :], ACT.Identity,
                                                bias=col["L1_gnn_beta1"][:, c:c + 1], scale=col["L1_gnn_g1"][:, c:c + 1])
                last.then_inc(x2T_ready, 1)

            def F1(n, g):
                act.wait_ge(up_psum, n * FB + g + 1)
                for k in range(2):
                    f = 2 * g + k
                    last = nc.scalar.activation(gT[:, f, :], two([S1, G1, O1, T1][g])[:, k, :], ACT.Gelu,
                                                bias=col["L1_gnn_b1"][:, f:f + 1])
                last.then_inc(gT_ready, 1)

            all_graphs({"x0": x0, "q0": q0, "k0": k0, "v0": v0, "R0": R0, "S0": S0_, "T0": T0_, "o0": o0,
                        "N0": N0, "x1": x1_, "q1": q1, "k1": k1, "S1": S1_, "V1": V1_, "X1": X1, "F1": F1}, act.Fori)

        @block.vector
        def _(dve):
            dve.wait_ge(weights_loaded, 16 * len(wide))

            def stats(key, n, tile):
                st, mv, ve, _ = ln[key]
                stats_done, moments_done, var_ready, _ = ln_sem[key]
                for t in range(T):
                    last = nc.vector.bn_stats(st[:, t, :], tile[:, t, :])
                last.then_inc(stats_done, 1)
                dve.wait_ge(stats_done, n + 1)
                at = U + list(ln).index(key)
                nc.vector.memset(held[:, at:at + 1], 0.0)
                for t in range(T):
                    last = nc.vector.bn_aggr(mv[:, t, :], st[:, t, :])
                last.then_inc(moments_done, 1)
                dve.wait_ge(moments_done, n + 1)
                nc.vector.tensor_scalar_add(ve[:, :], mv[:, :, 1], EPS).then_inc(var_ready, 1)

            def normalise(key, n, dst, src, done):
                _, mv, _, rs = ln[key]
                dve.wait_ge(ln_sem[key][3], n + 1)
                for t in range(T):
                    last = nc.vector.tensor_scalar(dst[:, t, :], src[:, t, :], mv[:, t, 0:1], rs[:, t:t + 1],
                                                   ALU.subtract, ALU.mult)
                last.then_inc(done, 1)

            def low(dst, bank_, high, bias=None):
                if bias is None:
                    return nc.vector.tensor_tensor(dst[:, :, :], two(bank_), high[:, :, :].bitcast(F32), ALU.subtract)
                for c in range(C):
                    last = nc.vector.scalar_tensor_tensor(dst[:, c, :], two(bank_)[:, c, :], bias[:, c:c + 1],
                                                          high[:, c, :].bitcast(F32), ALU.add, ALU.subtract)
                return last

            def q0(n):
                dve.wait_ge(qh0_ready, n + 1)
                low(ql0, S0, qh0).then_inc(q0_ready, 1)

            def k0(n):
                dve.wait_ge(kh0_ready, n + 1)
                low(kl0, G0, kh0).then_inc(k0_ready, 1)

            def q1(n):
                dve.wait_ge(qh1_ready, n + 1)
                low(ql1, S1, qh1, bqs).then_inc(q1_ready, 1)

            def k1(n):
                dve.wait_ge(kh1_ready, n + 1)
                low(kl1, G1, kh1, col["L1_gnn_bk"]).then_inc(k1_ready, 1)

            def m0(n):
                dve.wait_ge(adj_loaded, 16 * (n + 1))
                nc.vector.tensor_scalar(negm[:, :, :], adj_in[:, :, :], 0.0, NEG, ALU.is_le, ALU.mult)\
                    .then_inc(negm_ready, 1)

            def adj0(n):
                if later(n):
                    dve.wait_ge(adjT_psum, n)
                nc.vector.tensor_copy(adjb[:, :, :], adj_in[:, :, :]).then_inc(adjb_ready, 1)

            def S0_(n, u):
                dve.wait_ge(relu0_ready, n * U + u + 1)
                nc.vector.memset(held[:, u:u + 1], 0.0)
                for k in range(2):
                    pb = P0[:, u % 2, k, :]
                    last = nc.vector.tensor_tensor_reduce(out=pb, in0=two([S0, G0][u % 2])[:, k, :], in1=pb,
                                                          scale=-1.0, scalar=BIG, op0=ALU.add, op1=ALU.min,
                                                          accum_out=nb0[:, u, k:k + 1])
                last.then_inc(leaky0_ready, 1)

            def O0_(n):
                dve.wait_ge(exp0_ready, n * U + U)
                nc.vector.reciprocal(rinv0[:, :, :], sum0[:, :, :]).then_inc(rinv0_ready, 1)
                dve.wait_ge(rinv0_ready, n + 1)
                dve.wait_ge(o0_psum, n + 1)
                nc.vector.tensor_tensor(h0[:, :, :].rearrange("p t (h d) -> p (t h) d", d=DH),
                                        S0[:, :].rearrange("p (a d) -> p a d", d=DH),
                                        rinv0[:, :, :].rearrange("p t (h o) -> p (t h) o", o=1).to_broadcast([P, T * H, DH]),
                                        ALU.mult).then_inc(h0_ready, 1)
                dve.wait_ge(h0_ready, n + 1)
                stats("a0", n, h0)

            def N0(n):
                normalise("a0", n, h0, h0, z0_ready)

            def F0(n):
                dve.wait_ge(ffn0_psum, n + 1)
                stats("b0", n, two(G0))

            def Y0(n):
                if later(n):
                    dve.wait_ge(x1_ready, n)
                normalise("b0", n, y0, two(G0), y0_ready)

            def m1(n):
                dve.wait_ge(adjT_psum, n + 1)
                aT = O1[:, 0:N].bitcast(BF16).rearrange("p (j i) -> p j i", j=T)
                for r in range(R):
                    last = nc.vector.tensor_scalar(M1[:, r, :, :], aT, float(r), None, ALU.is_equal)
                last.then_inc(mask_ready, 1)

            def v1(n, r):
                dve.wait_ge(v1_psum, n * R + r + 1)
                nc.vector.tensor_tensor(V1[:, r, :, :], two([T1, O1][r % 2]), bv[:, r, :, :].to_broadcast([P, T, D]),
                                        ALU.add).then_inc(v1_ready, 1)

            def S1_(n, u):
                dve.wait_ge(scores1, n * U + u + 1)
                nc.vector.tensor_reduce(nb1[:, u, :], two([S1, G1][u % 2]), AX.X, ALU.max, negate=True)\
                    .then_inc(bias1_ready, 1)

            def T1_(n, u):
                c, q, t = unit(u)
                dve.wait_ge(pT1_psum, n * U + u + 1)
                if u == 0:
                    dve.wait_ge(mask_ready, n + 1)
                for r in range(R):
                    if u == 4:
                        dve.wait_ge(av1_psum, n * C * R + r + 1)
                    last = nc.vector.tensor_tensor(A1[:, r, q:q + 2, :, P * t:P * t + P],
                                                   T1[:, :].rearrange("p (k j i) -> p k j i", k=2, j=T),
                                                   M1[:, r:r + 1, :, P * t:P * t + P].to_broadcast([P, 2, T, P]),
                                                   ALU.mult)
                last.then_inc(A1_ready, 1)

            def V1_(n):
                dve.wait_ge(exp1_ready, n * U + U)
                nc.vector.reciprocal(rinv1[:, :, 0], sum1[:, :, :].rearrange("p t h -> p (t h)")).then_inc(rinv1_ready, 1)
                dve.wait_ge(rinv1_ready, n + 1)
                nc.vector.tensor_copy(rsp1[:, :, :].rearrange("p t (h d) -> p (t h) d", d=DH),
                                      rinv1[:, :, :].to_broadcast([P, T * H, DH])).then_inc(rsp1_ready, 1)

            def W1(n):
                dve.wait_ge(oT1_ready, n + 1)
                dve.wait_ge(rT1_psum, n + 1)
                nc.vector.tensor_tensor(at1[:, :, :], two(S1), oT1[:, :, :], ALU.mult).then_inc(at1_ready, 1)

            def r1_(n):
                dve.wait_ge(wo1_psum, n + 1)
                dve.wait_ge(x1b_ready, n + 1)
                if later(n):
                    dve.wait_ge(x2T_psum, n)
                    dve.wait_ge(n1g_ready, n)
                nc.vector.tensor_tensor(r1[:, :, :], two(G1), x1b[:, :, :], ALU.add).then_inc(r1_ready, 1)
                dve.wait_ge(r1_ready, n + 1)
                stats("a1", n, r1)

            def X1(n):
                normalise("a1", n, r1, r1, n1_ready)

            def r2_(n):
                dve.wait_ge(down_psum, n + 1)
                dve.wait_ge(x2b_ready, n + 1)
                if later(n):
                    dve.wait_ge(out_ready, n)
                nc.vector.tensor_tensor(r2[:, :, :], two(O1), x2b[:, :, :], ALU.add).then_inc(r2_ready, 1)
                dve.wait_ge(r2_ready, n + 1)
                stats("b1", n, r2)

            def Y1(n):
                normalise("b1", n, r2, r2, n2_ready)

            all_graphs({"m0": m0, "adj0": adj0, "q0": q0, "k0": k0, "S0": S0_, "O0": O0_, "N0": N0, "F0": F0,
                        "Y0": Y0, "m1": m1, "q1": q1, "k1": k1, "v1": v1, "S1": S1_, "T1": T1_, "V1": V1_,
                        "W1": W1, "r1": r1_, "X1": X1, "r2": r2_, "Y1": Y1}, dve.Fori)

        @block.tensor
        def _(pe):
            pe.wait_ge(ident_ready, 1)
            pe.wait_ge(weights_loaded, 16 * len(wide))
            for o in range(2 * C):
                if o >= 2:
                    pe.wait_ge(wf_ready, o - 1)
                for c in range(C):
                    last = nc.tensor.transpose([S0, G0][o % 2][:, P * c:P * c + P],
                                               wf0_in[:, c, P * o:P * o + P], ident[:, :])
                last.then_inc(wfT_psum, 1)
            pe.wait_ge(wf_ready, 2 * C)
            pe.wait_ge(identb_ready, 1)

            def mm(out_, lhsT, rhs, start, stop):
                return nc.tensor.matmul(out_, lhsT, rhs, start=start, stop=stop)

            def flip(bank_, tile):
                for a in range(2):
                    for b in range(2):
                        last = nc.tensor.transpose(two(bank_)[:, a, P * b:P * b + P],
                                                   tile[:, b, P * a:P * a + P], ident[:, :])
                return last

            def channels(bank_, weight, xT, cols=0):
                for o in range(2):
                    for c in range(C):
                        last = mm(two(bank_)[:, o, :], weight[:, c, cols + P * o:cols + P * o + P], xT[:, c, :],
                                  c == 0, c == C - 1)
                return last

            def nodes(bank_, pairs):
                for t in range(T):
                    for k, (xT, weight) in enumerate(pairs):
                        last = mm(two(bank_)[:, t, :], xT[:, P * t:P * t + P], weight, k == 0, k == len(pairs) - 1)
                return last

            def x0(n):
                pe.wait_ge(x_loaded, 16 * (n + 1))
                if later(n):
                    pe.wait_ge(zf0_ready, n)
                flip(T0, x_in).then_inc(xT0_psum, 1)

            def q0(n):
                pe.wait_ge(xT0_ready, n + 1)
                if later(n):
                    pe.wait_ge(h0_ready, n)
                channels(S0, wq0, xT0).then_inc(q0_psum, 1)

            def k0(n):
                if later(n):
                    pe.wait_ge(y0_ready, n)
                channels(G0, wk0, xT0).then_inc(k0_psum, 1)

            def v0(n):
                pe.wait_ge(xT0_ready, n + 1)
                if later(n):
                    pe.wait_ge(oT0_ready, n)
                nodes(O0, [(xT0[:, c, :], wv0[:, c, :]) for c in range(C)]).then_inc(v0_psum, 1)

            def R0(n, u):
                c, q, t = unit(u)
                if u == 0:
                    pe.wait_ge(q0_stacked, (n + 1) * STACKS)
                    pe.wait_ge(k0_stacked, (n + 1) * STACKS)
                    pe.wait_ge(negm_ready, n + 1)
                if u >= 2:
                    pe.wait_ge(leaky0_ready, n * U + u - 1)
                b = [S0, G0][u % 2]
                mm(two(b), identb[:, :], negm[:, t:t + 1, :].to_broadcast([P, 2, N]), True, False)
                for k in range(2):
                    last = mm(two(b)[:, k, :], Qs0[:, q + k, c, P * t:P * t + P], Ks0[:, q + k, c, :], False, k == 1)
                last.then_inc(scores0, 1)

            def blocks(bank_, probs):
                for k in range(2):
                    for j in range(T):
                        at = P * (T * k + j)
                        last = nc.tensor.transpose(bank_[:, at:at + P], probs[:, k, P * j:P * j + P], ident[:, :])
                return last

            def T0_(n, u):
                pe.wait_ge(exp0_ready, n * U + u + 1)
                if u:
                    pe.wait_ge(PT0_ready, n * U + u)
                blocks(T0, P0[:, u % 2, :, :]).then_inc(pT0_psum, 1)

            def A0(n, c):
                pe.wait_ge(PT0_ready, n * U + 4 * c + 4)
                if c == 0:
                    pe.wait_ge(v0_ready, n + 1)
                for j in range(T):
                    for q in range(Q):
                        h = Q * c + q
                        last = mm(two(O0)[DH * q:DH * q + DH, c, :], V0[:, j, DH * h:DH * h + DH],
                                  PT0[:, q, j, :], j == 0, j == T - 1)
                last.then_inc(av0_psum, 1)

            def o0(n):
                pe.wait_ge(oT0_ready, n + 1)
                pe.wait_ge(leaky0_ready, n * U + U - 1)
                flip(S0, oT0).then_inc(o0_psum, 1)

            def N0(n):
                pe.wait_ge(z0_ready, n + 1)
                pe.wait_ge(PT0_ready, n * U + U)
                flip(T0, h0).then_inc(zT0_psum, 1)

            def F0(n):
                pe.wait_ge(zf0_ready, n + 1)
                pe.wait_ge(leaky0_ready, n * U + U)
                nodes(G0, [(zf0[:, c, :], wf0[:, c, :]) for c in range(C)] +
                      [(xT0[:, c, :], wf0[:, C + c, :]) for c in range(C)]).then_inc(ffn0_psum, 1)

            def x1_(n):
                pe.wait_ge(x1_ready, n + 1)
                if later(n):
                    pe.wait_ge(A1_ready, n * U)
                flip(T1, x1).then_inc(xT1_psum, 1)

            def m1(n):
                pe.wait_ge(adjb_ready, n + 1)
                if later(n):
                    pe.wait_ge(oT1_ready, n)
                ob = O1[:, 0:N].bitcast(BF16)
                for j in range(T):
                    for t in range(T):
                        at = N * j + P * t
                        last = nc.tensor.transpose(ob[:, at:at + P], adjb[:, t, P * j:P * j + P], identb[:, :])
                last.then_inc(adjT_psum, 1)

            def q1(n):
                pe.wait_ge(xT1_ready, n + 1)
                if later(n):
                    pe.wait_ge(exp1_ready, n * U - 1)
                channels(S1, wq1, xT1).then_inc(q1_psum, 1)

            def k1(n):
                if later(n):
                    pe.wait_ge(exp1_ready, n * U)
                channels(G1, wk1, xT1).then_inc(k1_psum, 1)

            def v1(n, r):
                if r == 0:
                    pe.wait_ge(xT1_ready, n + 1)
                elif r == 1:
                    pe.wait_ge(mask_ready, n + 1)
                else:
                    pe.wait_ge(v1_ready, n * R + r - 1)
                nodes([T1, O1][r % 2], [(xT1[:, c, :], wv1[:, r, c, :]) for c in range(C)]).then_inc(v1_psum, 1)

            def S1_(n, u):
                c, q, t = unit(u)
                if u == 0:
                    pe.wait_ge(q1_stacked, (n + 1) * STACKS)
                    pe.wait_ge(k1_stacked, (n + 1) * STACKS)
                if u < 2 and later(n):
                    pe.wait_ge(gT_ready, (n - 1) * FB + u + 1)
                if u >= 2:
                    pe.wait_ge(exp1_ready, n * U + u - 1)
                for k in range(2):
                    last = mm(two([S1, G1][u % 2])[:, k, :], Qs1[:, q + k, c, P * t:P * t + P], Ks1[:, q + k, c, :],
                              True, True)
                last.then_inc(scores1, 1)

            def T1_(n, u):
                pe.wait_ge(exp1_ready, n * U + u + 1)
                if u:
                    pe.wait_ge(A1_ready, n * U + u)
                else:
                    pe.wait_ge(v1_ready, n * R + R - 1)
                    if later(n):
                        pe.wait_ge(gT_ready, n * FB)
                blocks(T1, P1[:, u % 2, :, :]).then_inc(pT1_psum, 1)

            def A1_(n, c):
                pe.wait_ge(A1_ready, n * U + 4 * c + 4)
                if c == 0:
                    pe.wait_ge(v1_ready, n * R + R)
                    if later(n):
                        pe.wait_ge(r2_ready, n)
                for r in range(R):
                    for j in range(T):
                        for q in range(Q):
                            h = Q * c + q
                            last = mm(two(O1)[DH * q:DH * q + DH, c, :], V1[:, r, j, DH * h:DH * h + DH],
                                      A1[:, r, q, j, :], r == 0 and j == 0, r == R - 1 and j == T - 1)
                    last.then_inc(av1_psum, 1)

            def V1_(n):
                pe.wait_ge(rsp1_ready, n + 1)
                if last_graph(n, G):
                    pe.wait_ge(exp1_ready, n * U + U - 1)
                else:
                    pe.wait_ge(q1_ready, n + 2)
                flip(S1, rsp1).then_inc(rT1_psum, 1)

            def W1(n):
                pe.wait_ge(at1_ready, n + 1)
                if last_graph(n, G):
                    pe.wait_ge(exp1_ready, n * U + U)
                else:
                    pe.wait_ge(k1_ready, n + 2)
                nodes(G1, [(at1[:, c, :], wo1[:, c, :]) for c in range(C)]).then_inc(wo1_psum, 1)

            def X1(n):
                pe.wait_ge(n1_ready, n + 1)
                if last_graph(n, G):
                    pe.wait_ge(A1_ready, n * U + U)
                else:
                    pe.wait_ge(v1_ready, (n + 2) * R - 1)
                flip(T1, r1).then_inc(x2T_psum, 1)

            def F1(n, g):
                if g == 0:
                    pe.wait_ge(at1_ready, n + 1)
                    pe.wait_ge(x2T_ready, n + 1)
                elif g == 1:
                    pe.wait_ge(r1_ready, n + 1)
                elif g == 2 and last_graph(n, G):
                    pe.wait_ge(oT1_ready, n + 1)
                elif g == 2:
                    pe.wait_ge(v1_ready, (n + 2) * R)
                channels([S1, G1, O1, T1][g], w1, x2T, cols=2 * P * g).then_inc(up_psum, 1)

            def F2(n):
                pe.wait_ge(gT_ready, n * FB + FB)
                nodes(O1, [(gT[:, f, :], w2[:, f, :]) for f in range(FC)]).then_inc(down_psum, 1)

            all_graphs({"x0": x0, "q0": q0, "k0": k0, "v0": v0, "R0": R0, "T0": T0_, "A0": A0, "o0": o0,
                            "N0": N0, "F0": F0, "x1": x1_, "m1": m1, "q1": q1, "k1": k1, "v1": v1, "S1": S1_,
                            "T1": T1_, "A1": A1_, "V1": V1_, "W1": W1, "X1": X1, "F1": F1, "F2": F2}, pe.Fori)


WEIGHTS = ["L0_gnn_Wq", "L0_gnn_Wk", "L0_gnn_Wv", "L0_gnn_Wffn", "L0_gnn_g1", "L0_gnn_b1", "L0_gnn_g2",
           "L0_gnn_b2", "L1_gnn_Wq", "L1_gnn_bq", "L1_gnn_Wk", "L1_gnn_bk", "L1_gnn_Wv", "L1_gnn_bv",
           "L1_gnn_Wo", "L1_gnn_bo", "L1_gnn_W1", "L1_gnn_b1", "L1_gnn_W2", "L1_gnn_b2", "L1_gnn_g1",
           "L1_gnn_beta1", "L1_gnn_g2", "L1_gnn_beta2"]


def kernel(**inputs):
    import numpy as _np
    import concourse.bacc as _bacc
    from concourse import mybir as _mybir
    from concourse.bass_utils import run_bass_kernel_spmd as _run

    nc = _bacc.Bacc("TRN2", target_bir_lowering=False, num_devices=1)
    arrays, aps = {}, {}
    for name in ["x", "adj"] + WEIGHTS:
        a = _np.ascontiguousarray(inputs[name])
        arrays[f"in_{name}"] = a
        aps[name] = nc.dram_tensor(f"in_{name}", a.shape, _mybir.dt.from_np(a.dtype), kind="ExternalInput").ap()
    out = nc.dram_tensor("out_x", arrays["in_x"].shape, _mybir.dt.float32, kind="ExternalOutput").ap()
    graph_layers_kernel(nc, aps["x"], aps["adj"], {name: aps[name] for name in WEIGHTS}, out)
    r = _run(nc, [arrays], core_ids=[0])
    return r.results[0]["out_x"]
```

```python
from contextlib import ExitStack

import concourse.bass as bass
from concourse import mybir

F32 = mybir.dt.float32
F32R = mybir.dt.float32r
BF16 = mybir.dt.bfloat16
I32 = mybir.dt.int32
ALU = mybir.AluOpType
ACT = mybir.ActivationFunctionType
AX = mybir.AxisListType

P = 128
D = 256
N = 256
C = D // P
T = N // P
H, DH = 8, 32
Q = P // DH
STACKS = 3 * Q // 2 * 16
ST = 3 * DH
R = 4
FF = 1024
FC = FF // P
FB = FC // 2
U = H * T // 2
NEG = -float(2 ** 53)
SLOPE = 0.2
EPS = 1e-5
BIG = 3e38
SCALE = float(DH) ** -0.5


def unit(u):
    return u // 4, 2 * (u % 4 // 2), u % 2


def later(n):
    return not (isinstance(n, int) and n == 0)


ORDER_TEXT = """
T0.7/1 S1.0/2 S1.1/2 v1.3/2 A0.1/1 e0/1 o0/1 X1/3 O0/1 T1.0/2 b1/2 F1.0/3 N0/1 S1.2/2 S1.3/2 T1.1/2
F1.1/3 h1/2 load_adj/0 L0.0/1 L0.1/1 F0/1 T1.2/2 x0/0 load_x/0 F1.2/3 T1.3/2 k0/0 F1.3/3 Y0/1 S1.4/2
S1.5/2 m0/0 A1.0.0/2 q0/0 A1.0.1/2 T1.4/2 S1.6/2 A1.0.2/2 S1.7/2 A1.0.3/2 T1.5/2 F2.0/3 v0/0 T1.6/2
F2.1/3 T1.7/2 R0.0/0 S0.0/0 F2.2/3 F2.3/3 R0.1/0 S0.1/0 x1/1 A1.1.0/2 T0.0/0 A1.1.1/2 R0.2/0 r2/3
A1.1.2/2 T0.1/0 A1.1.3/2 V1/2 R0.3/0 h0/0 Y1/3 S0.2/0 S0.3/0 Z1/2 m1/1 k1/1 R0.4/0 T0.2/0 S0.4/0 q1/1
T0.3/0 R0.5/0 v1.0/1 A0.0/0 T0.4/0 R0.6/0 S0.5/0 W1/2 S0.6/0 R0.7/0 r1/2 T0.5/0 S0.7/0 v1.1/1 T0.6/0
v1.2/1 adj0/0
"""
ORDER = [(name.split(".")[0], *map(int, name.split(".")[1:]), int(lag))
         for name, lag in (entry.split("/") for entry in ORDER_TEXT.split())]
LAG = max(s[-1] for s in ORDER)


def graph_layers_kernel(nc, x, adj, w, out):
    G = x.shape[0]
    ctx = ExitStack()
    with ctx:
        def sb(name, shape, dt=F32):
            return ctx.enter_context(nc.sbuf_tensor(name, shape, dt))

        def bank(name):
            return ctx.enter_context(nc.psum_tensor(name, [P, 512], F32))

        def sem(name):
            return ctx.enter_context(nc.semaphore(name))

        ident = sb("ident", [P, P])
        identb = sb("identb", [P, P], BF16)
        wq0, wk0, wv0 = (sb(f"w{a}0_sb", [P, C, D]) for a in "qkv")
        wf0 = sb("wf0", [P, 2 * C, D])
        wq1, wk1, wo1 = (sb(f"w{a}1_sb", [P, C, D]) for a in "qko")
        wv1 = sb("wv1_sb", [P, R, C, D])
        w1 = sb("w1_sb", [P, C, FF])
        w2 = sb("w2_sb", [P, FC, D])
        rep = {name: sb(f"rep_{name}", [P, 1, D]) for name in
               ("L0_gnn_g2", "L0_gnn_b2", "L1_gnn_bo", "L1_gnn_g1", "L1_gnn_beta1",
                "L1_gnn_g2", "L1_gnn_beta2")}
        bv = sb("bv_rep", [P, R, 1, D])
        col = {name: sb(f"col_{name}", [P, n]) for name, n in
               (("L0_gnn_g1", C), ("L0_gnn_b1", C), ("L1_gnn_bq", C), ("L1_gnn_bk", C), ("L1_gnn_b1", FC),
                ("L1_gnn_g1", C), ("L1_gnn_beta1", C))}
        minus_half = sb("minus_half", [P, T])
        held = sb("held", [P, U + 4])
        bqs = sb("bqs", [P, C])

        x_in = sb("x_in", [P, T, D])
        adj_in = sb("adj_in", [P, T, N], I32)
        xb = sb("xb", [P, T, D])
        negm = sb("negm", [P, T, N], BF16)
        adjb = sb("adjb", [P, T, N], BF16)
        xT0 = sb("xT0", [P, C, N])
        qh0, ql0, kh0, kl0 = (sb(a, [P, C, N], F32R) for a in ("qh0", "ql0", "kh0", "kl0"))
        Qs0, Ks0 = (sb(a, [ST, Q, C, N], F32R) for a in ("Qs0", "Ks0"))
        V0 = sb("V0", [P, T, D])
        P0 = sb("P0", [P, 2, 2, N])
        PT0 = sb("PT0", [P, Q, T, N])
        nb0 = sb("nb0", [P, U, 2])
        sum0 = sb("sum0", [P, T, H])
        rinv0 = sb("rinv0", [P, T, H])
        oT0 = sb("oT0", [P, C, N])
        h0 = sb("h0", [P, T, D])
        zf0 = sb("zf0", [P, C, N])
        y0 = h0
        x1 = sb("x1", [P, T, D])
        x1b = sb("x1b", [P, T, D])
        xT1 = sb("xT1", [P, C, N])
        M1 = sb("M1", [P, R, T, N], BF16)
        qh1, ql1, kh1, kl1 = (sb(a, [P, C, N], F32R) for a in ("qh1", "ql1", "kh1", "kl1"))
        Qs1, Ks1 = (sb(a, [ST, Q, C, N], F32R) for a in ("Qs1", "Ks1"))
        V1 = sb("V1", [P, R, T, D])
        P1 = sb("P1", [P, 2, 2, N])
        PT1 = sb("PT1", [P, 2, 2, T, P])
        A1 = sb("A1", [P, R, Q, T, N])
        nb1 = sb("nb1", [P, U, 2])
        sum1 = sb("sum1", [P, T, H])
        rinv1 = sb("rinv1", [P, T * H, 1])
        r1 = sb("r1", [P, T, D])
        rsp1 = r1
        x2b = sb("x2b", [P, T, D])
        gT = sb("gT", [P, FC, N])
        oT1, at1 = (sb(a, [P, C, N]) for a in ("oT1", "at1"))
        x2T = at1
        wf0_in = gT[:, 0:4, :].rearrange("p (c a) n -> p c (a n)", c=C)
        r2 = sb("r2", [P, T, D])
        out_tok = r2
        ln = {k: (sb(f"st_{k}", [P, T, 6]), sb(f"mv_{k}", [P, T, 2]), sb(f"ve_{k}", [P, T]),
                  sb(f"rs_{k}", [P, T])) for k in ("a0", "b0", "a1", "b1")}
        ln_sem = {k: (sem(f"stats_{k}"), sem(f"moments_{k}"), sem(f"var_{k}_ready"), sem(f"rstd_{k}_ready"))
                  for k in ln}

        S0, G0, T0, O0 = bank("S0"), bank("G0"), bank("T0"), bank("O0")
        S1, G1, T1, O1 = bank("S1"), bank("G1"), bank("T1"), bank("O1")

        def two(b):
            return b[:, :].rearrange("p (a n) -> p a n", a=2)

        weights_loaded = sem("weights_loaded")
        cols_loaded = sem("cols_loaded")
        zeroed = sem("zeroed")
        ident_ready = sem("ident_ready")
        identb_ready = sem("identb_ready")
        half_ready = sem("half_ready")
        bqs_ready = sem("bqs_ready")
        wfT_psum = sem("wfT_psum")
        wf_ready = sem("wf_ready")
        x_loaded, adj_loaded, out_stored = sem("x_loaded"), sem("adj_loaded"), sem("out_stored")
        xT0_psum, xT0_ready, xb_ready = sem("xT0_psum"), sem("xT0_ready"), sem("xb_ready")
        negm_ready, adjb_ready = sem("negm_ready"), sem("adjb_ready")
        q0_psum, q0_ready, k0_psum, k0_ready = sem("q0_psum"), sem("q0_ready"), sem("k0_psum"), sem("k0_ready")
        qh0_ready, kh0_ready, qh1_ready, kh1_ready = (sem(a + "_ready") for a in ("qh0", "kh0", "qh1", "kh1"))
        q0_stacked, k0_stacked, q1_stacked, k1_stacked = ([sem(f"{a}_stacked_{half}") for half in range(2)]
                                                          for a in ("q0", "k0", "q1", "k1"))
        v0_psum, v0_ready = sem("v0_psum"), sem("v0_ready")
        scores0, relu0_ready = sem("scores0"), sem("relu0_ready")
        leaky0_ready, exp0_ready = sem("leaky0_ready"), sem("exp0_ready")
        pT0_psum, PT0_ready, av0_psum = sem("pT0_psum"), sem("PT0_ready"), sem("av0_psum")
        oT0_ready, o0_psum = sem("oT0_ready"), sem("o0_psum")
        rinv0_ready, h0_ready = sem("rinv0_ready"), sem("h0_ready")
        z0_ready, zT0_psum, zf0_ready = sem("z0_ready"), sem("zT0_psum"), sem("zf0_ready")
        ffn0_psum, y0_ready, y0g_ready, x1_ready = sem("ffn0_psum"), sem("y0_ready"), sem("y0g_ready"), sem("x1_ready")
        xT1_psum, xT1_ready, x1b_ready = sem("xT1_psum"), sem("xT1_ready"), sem("x1b_ready")
        adjT_psum, mask_ready = sem("adjT_psum"), sem("mask_ready")
        q1_psum, q1_ready, k1_psum, k1_ready = sem("q1_psum"), sem("q1_ready"), sem("k1_psum"), sem("k1_ready")
        v1_psum, v1_ready = sem("v1_psum"), sem("v1_ready")
        scores1, bias1_ready, exp1_ready = sem("scores1"), sem("bias1_ready"), sem("exp1_ready")
        pT1_psum, A1_ready, av1_psum = sem("pT1_psum"), sem("A1_ready"), sem("av1_psum")
        PT1_ready, A13_ready = sem("PT1_ready"), sem("A13_ready")
        oT1_ready, rinv1_ready, rsp1_ready = sem("oT1_ready"), sem("rinv1_ready"), sem("rsp1_ready")
        rT1_psum, at1_ready = sem("rT1_psum"), sem("at1_ready")
        wo1_psum, r1_ready, n1_ready, n1g_ready = sem("wo1_psum"), sem("r1_ready"), sem("n1_ready"), sem("n1g_ready")
        x2b_ready, x2T_psum, x2T_ready = sem("x2b_ready"), sem("x2T_psum"), sem("x2T_ready")
        up_psum, gT_ready = sem("up_psum"), sem("gT_ready")
        down_psum, r2_ready, n2_ready = sem("down_psum"), sem("r2_ready"), sem("n2_ready")
        n2g_ready, out_ready = sem("n2g_ready"), sem("out_ready")

        def chunks(a):
            return a.rearrange("(c p) o -> p c o", p=P)

        wide = [(wq0[:, :, :], chunks(w["L0_gnn_Wq"])), (wk0[:, :, :], chunks(w["L0_gnn_Wk"])),
                (wv0[:, :, :], chunks(w["L0_gnn_Wv"])), (wf0_in[:, :, :], chunks(w["L0_gnn_Wffn"])),
                (wq1[:, :, :], chunks(w["L1_gnn_Wq"])), (wk1[:, :, :], chunks(w["L1_gnn_Wk"])),
                (wo1[:, :, :], chunks(w["L1_gnn_Wo"])), (w1[:, :, :], chunks(w["L1_gnn_W1"])),
                (w2[:, :, :], chunks(w["L1_gnn_W2"]))]
        wide += [(wv1[:, r, :, :], chunks(w["L1_gnn_Wv"][r])) for r in range(R)]
        wide += [(rep[name][:, 0, :], w[name].partition_broadcast(P)) for name in rep]
        wide += [(x2b[:, 0, :], w["L1_gnn_b2"].partition_broadcast(P))]
        wide += [(bv[:, r, 0, :], w["L1_gnn_bv"][r].partition_broadcast(P)) for r in range(R)]
        narrow = [(col[name][:, :], w[name].rearrange("(c p) -> p c", p=P)) for name in col]
        x_v = x.rearrange("g (t p) d -> g p t d", p=P)
        adj_v = adj.rearrange("g (t p) m -> g p t m", p=P)
        out_v = out.rearrange("g (t p) d -> g p t d", p=P)

        def graph(view, n):
            if isinstance(n, int):
                return view[n]
            return view[bass.ds(n, 1)].rearrange("g p t d -> (g p) t d")

        def run_stages(stages, i):
            for name, *k, lag in ORDER:
                if name in stages and not (isinstance(i, int) and not 0 <= i - lag < G):
                    stages[name](i - lag, *k)

        def all_graphs(stages, fori):
            for i in range(LAG + 1):
                run_stages(stages, i)
            with fori(LAG + 1, G) as i:
                run_stages(stages, i)
            for i in range(G, G + LAG):
                run_stages(stages, i)

        block = ctx.enter_context(nc.Block())

        def by_relation(engine, u, r):
            c, q, t = unit(u)
            return engine.tensor_tensor(A1[:, r, q:q + 2, :, P * t:P * t + P], PT1[:, u % 2, :, :, :],
                                        M1[:, r:r + 1, :, P * t:P * t + P].to_broadcast([P, 2, T, P]), ALU.mult)

        @block.sync
        def _(sp):
            for dst, src in wide:
                sp.dma_start(dst, src).then_inc(weights_loaded, 16)

            def load_x(n):
                if later(n):
                    sp.wait_ge(xT0_psum, n)
                    sp.wait_ge(xb_ready, n)
                sp.dma_start(x_in[:, :, :], graph(x_v, n)).then_inc(x_loaded, 16)

            def load_adj(n):
                if later(n):
                    sp.wait_ge(negm_ready, n)
                    sp.wait_ge(adjb_ready, n)
                sp.dma_start(adj_in[:, :, :], graph(adj_v, n)).then_inc(adj_loaded, 16)

            def stack(parts, dst, done, half):
                for q in range(Q // 2 * half, Q // 2 * half + Q // 2):
                    for b, part in enumerate(parts):
                        sp.dma_start(dst[DH * b:DH * b + DH, q, :, :].bitcast(F32),
                                     part[DH * q:DH * q + DH, :, :].bitcast(F32)).then_inc(done[half], 16)

            def q0(n):
                sp.wait_ge(q0_ready, n + 1)
                stack((qh0, ql0, qh0), Qs0, q0_stacked, 0)

            def k0(n):
                sp.wait_ge(k0_ready, n + 1)
                stack((kh0, kh0, kl0), Ks0, k0_stacked, 0)

            def h0_(n):
                sp.wait_ge(q0_ready, n + 1)
                sp.wait_ge(k0_ready, n + 1)
                stack((qh0, ql0, qh0), Qs0, q0_stacked, 1)
                stack((kh0, kh0, kl0), Ks0, k0_stacked, 1)

            def q1(n):
                sp.wait_ge(q1_ready, n + 1)
                stack((qh1, ql1, qh1), Qs1, q1_stacked, 0)

            def k1(n):
                sp.wait_ge(k1_ready, n + 1)
                stack((kh1, kh1, kl1), Ks1, k1_stacked, 0)

            def h1(n):
                sp.wait_ge(q1_ready, n + 1)
                sp.wait_ge(k1_ready, n + 1)
                stack((qh1, ql1, qh1), Qs1, q1_stacked, 1)
                stack((kh1, kh1, kl1), Ks1, k1_stacked, 1)

            def Y1(n):
                sp.wait_ge(out_ready, n + 1)
                sp.dma_start(graph(out_v, n), out_tok[:, :, :]).then_inc(out_stored, 16)

            all_graphs({"load_x": load_x, "load_adj": load_adj, "q0": q0, "k0": k0, "h0": h0_,
                        "q1": q1, "k1": k1, "h1": h1, "Y1": Y1},
                       sp.Fori)
            sp.wait_ge(out_stored, 16 * G)

        @block.gpsimd
        def _(pool):
            nc.gpsimd.memset(minus_half[:, :], -0.5).then_inc(half_ready, 1)
            nc.gpsimd.memset(ident[:, :], 0.0).then_inc(zeroed, 1)
            pool.wait_ge(zeroed, 1)
            nc.gpsimd.affine_select(out=ident[:, :], in_=ident[:, :], compare_op=ALU.not_equal, fill=1.0,
                                    base=0, pattern=[[-1, P]], channel_multiplier=1).then_inc(ident_ready, 1)
            pool.wait_ge(half_ready, 1)
            pool.wait_ge(weights_loaded, 16 * len(wide))

            nc.gpsimd.tensor_tensor(rep["L1_gnn_beta1"][:, :, :], rep["L1_gnn_beta1"][:, :, :],
                                    x2b[:, 0:1, :], ALU.add).then_inc(zeroed, 1)
            pool.wait_ge(zeroed, 2)

            def vec(name):
                return rep[name][:, :, :].to_broadcast([P, T, D])

            def rstd(key, n):
                _, _, var, rs = ln[key]
                _, _, var_ready, rstd_ready = ln_sem[key]
                pool.wait_ge(var_ready, n + 1)
                nc.gpsimd.tensor_tensor(rs[:, :], var[:, :], minus_half[:, :], ALU.pow).then_inc(rstd_ready, 1)

            def e0(n):
                pool.wait_ge(x_loaded, 16 * (n + 1))
                if later(n):
                    pool.wait_ge(x1_ready, n)
                nc.gpsimd.tensor_tensor(xb[:, :, :], x_in[:, :, :], vec("L0_gnn_b2"), ALU.add).then_inc(xb_ready, 1)

            def O0_(n):
                rstd("a0", n)

            def F0(n):
                rstd("b0", n)

            def Y0(n):
                pool.wait_ge(y0_ready, n + 1)
                nc.gpsimd.tensor_tensor(y0[:, :, :], y0[:, :, :], vec("L0_gnn_g2"), ALU.mult).then_inc(y0g_ready, 1)
                pool.wait_ge(y0g_ready, n + 1)
                pool.wait_ge(xb_ready, n + 1)
                if later(n):
                    pool.wait_ge(xT1_psum, n)
                    pool.wait_ge(x1b_ready, n)
                nc.gpsimd.tensor_tensor(x1[:, :, :], y0[:, :, :], xb[:, :, :], ALU.add).then_inc(x1_ready, 1)

            def b1(n):
                pool.wait_ge(x1_ready, n + 1)
                if later(n):
                    pool.wait_ge(r1_ready, n)
                nc.gpsimd.tensor_tensor(x1b[:, :, :], x1[:, :, :], vec("L1_gnn_bo"), ALU.add).then_inc(x1b_ready, 1)

            def T1_(n, u):
                pool.wait_ge(PT1_ready, n * U + u + 1)
                if u == 0:
                    pool.wait_ge(mask_ready, n + 1)
                if u == 4:
                    pool.wait_ge(av1_psum, n * C * R + R)
                by_relation(nc.gpsimd, u, R - 1).then_inc(A13_ready, 1)

            def r1_(n):
                rstd("a1", n)

            def X1(n):
                pool.wait_ge(n1_ready, n + 1)
                if later(n):
                    pool.wait_ge(r2_ready, n)
                nc.gpsimd.tensor_tensor(x2b[:, :, :], r1[:, :, :], vec("L1_gnn_g1"), ALU.mult).then_inc(n1g_ready, 1)
                pool.wait_ge(n1g_ready, n + 1)
                nc.gpsimd.tensor_tensor(x2b[:, :, :], x2b[:, :, :], vec("L1_gnn_beta1"), ALU.add).then_inc(x2b_ready, 1)

            def r2_(n):
                rstd("b1", n)

            def Y1(n):
                pool.wait_ge(n2_ready, n + 1)
                nc.gpsimd.tensor_tensor(r2[:, :, :], r2[:, :, :], vec("L1_gnn_g2"), ALU.mult).then_inc(n2g_ready, 1)
                pool.wait_ge(n2g_ready, n + 1)
                nc.gpsimd.tensor_tensor(out_tok[:, :, :], r2[:, :, :], vec("L1_gnn_beta2"), ALU.add)\
                    .then_inc(out_ready, 1)

            all_graphs({"e0": e0, "O0": O0_, "F0": F0, "Y0": Y0, "b1": b1, "T1": T1_, "r1": r1_, "X1": X1,
                        "r2": r2_, "Y1": Y1}, pool.Fori)

        @block.scalar
        def _(act):
            for dst, src in narrow:
                act.dma_start(dst, src, allow_slow_non_contiguous=True).then_inc(cols_loaded, 16)
            act.wait_ge(ident_ready, 1)
            nc.scalar.copy(identb[:, :], ident[:, :]).then_inc(identb_ready, 1)
            for o in range(2 * C):
                act.wait_ge(wfT_psum, o + 1)
                nc.scalar.copy(wf0[:, o, :], [S0, G0][o % 2][:, 0:D]).then_inc(wf_ready, 1)
            act.wait_ge(cols_loaded, 16 * len(narrow))
            nc.scalar.mul(bqs[:, :], col["L1_gnn_bq"][:, :], SCALE).then_inc(bqs_ready, 1)
            act.wait_ge(weights_loaded, 16 * len(wide))
            nc.scalar.mul(wq1[:, :, :], wq1[:, :, :], SCALE).then_inc(bqs_ready, 1)
            act.wait_ge(bqs_ready, 2)

            def x0(n):
                act.wait_ge(xT0_psum, n + 1)
                nc.scalar.copy(xT0[:, :, :], two(T0)).then_inc(xT0_ready, 1)

            def q0(n):
                act.wait_ge(q0_psum, n + 1)
                nc.scalar.copy(qh0[:, :, :], two(S0)).then_inc(qh0_ready, 1)

            def k0(n):
                act.wait_ge(k0_psum, n + 1)
                nc.scalar.copy(kh0[:, :, :], two(T0)).then_inc(kh0_ready, 1)

            def v0(n):
                act.wait_ge(v0_psum, n + 1)
                nc.scalar.copy(V0[:, :, :], two(O0)).then_inc(v0_ready, 1)

            def R0(n, u):
                act.wait_ge(scores0, n * U + u + 1)
                if u >= 2 or later(n):
                    act.wait_ge(pT0_psum, n * U + u - 1)
                nc.scalar.activation(P0[:, u % 2, :, :], two(S0), ACT.Relu, scale=SLOPE - 1.0)\
                    .then_inc(relu0_ready, 1)

            def S0_(n, u):
                c, q, t = unit(u)
                act.wait_ge(leaky0_ready, n * U + u + 1)
                pb = P0[:, u % 2, :, :]
                for k in range(2):
                    h = Q * c + q + k
                    last = nc.scalar.activation(pb[:, k, :], pb[:, k, :], ACT.Exp, bias=nb0[:, u, k:k + 1],
                                                scale=-1.0, accum_out=sum0[:, t, h:h + 1])
                last.then_inc(exp0_ready, 1)

            def T0_(n, u):
                c, q, t = unit(u)
                act.wait_ge(pT0_psum, n * U + u + 1)
                if u == 4:
                    act.wait_ge(av0_psum, n * C + 1)
                nc.scalar.copy(PT0[:, q:q + 2, :, P * t:P * t + P],
                               T0[:, :].rearrange("p (k j i) -> p k j i", k=2, j=T)).then_inc(PT0_ready, 1)

            def o0(n):
                act.wait_ge(av0_psum, n * C + C)
                nc.scalar.copy(oT0[:, :, :], two(O0)).then_inc(oT0_ready, 1)

            def N0(n):
                act.wait_ge(zT0_psum, n + 1)
                for c in range(C):
                    last = nc.scalar.activation(zf0[:, c, :], two(T0)[:, c, :], ACT.Identity,
                                                bias=col["L0_gnn_b1"][:, c:c + 1], scale=col["L0_gnn_g1"][:, c:c + 1])
                last.then_inc(zf0_ready, 1)

            def x1_(n):
                act.wait_ge(xT1_psum, n + 1)
                nc.scalar.copy(xT1[:, :, :], two(T1)).then_inc(xT1_ready, 1)

            def q1(n):
                act.wait_ge(q1_psum, n + 1)
                for c in range(C):
                    last = nc.scalar.activation(qh1[:, c, :], two(S1)[:, c, :], ACT.Identity, bias=bqs[:, c:c + 1])
                last.then_inc(qh1_ready, 1)

            def k1(n):
                act.wait_ge(k1_psum, n + 1)
                for c in range(C):
                    last = nc.scalar.activation(kh1[:, c, :], two(G1)[:, c, :], ACT.Identity,
                                                bias=col["L1_gnn_bk"][:, c:c + 1])
                last.then_inc(kh1_ready, 1)

            def S1_(n, u):
                c, q, t = unit(u)
                act.wait_ge(bias1_ready, n * U + u + 1)
                if u == 0 and later(n):
                    act.wait_ge(rinv1_ready, n)
                if u >= 2 or later(n):
                    act.wait_ge(pT1_psum, n * U + u - 1)
                for k in range(2):
                    h = Q * c + q + k
                    last = nc.scalar.activation(P1[:, u % 2, k, :], two([S1, G1][u % 2])[:, k, :], ACT.Exp,
                                                bias=nb1[:, u, k:k + 1],
                                                accum_out=sum1[:, t, h:h + 1])
                last.then_inc(exp1_ready, 1)

            def T1_(n, u):
                act.wait_ge(pT1_psum, n * U + u + 1)
                if u >= 2 or later(n):
                    act.wait_ge(A1_ready, n * U + u - 1)
                    act.wait_ge(A13_ready, n * U + u - 1)
                nc.scalar.copy(PT1[:, u % 2, :, :, :], T1[:, :].rearrange("p (k j i) -> p k j i", k=2, j=T))\
                    .then_inc(PT1_ready, 1)

            def V1_(n):
                act.wait_ge(av1_psum, (n * C + C) * R)
                if later(n):
                    act.wait_ge(at1_ready, n)
                nc.scalar.copy(oT1[:, :, :], two(O1)).then_inc(oT1_ready, 1)

            def X1(n):
                act.wait_ge(x2T_psum, n + 1)
                for c in range(C):
                    last = nc.scalar.activation(x2T[:, c, :], two(G0)[:, c, :], ACT.Identity,
                                                bias=col["L1_gnn_beta1"][:, c:c + 1], scale=col["L1_gnn_g1"][:, c:c + 1])
                last.then_inc(x2T_ready, 1)

            def F1(n, g):
                act.wait_ge(up_psum, n * FB + g + 1)
                for k in range(2):
                    f = 2 * g + k
                    last = nc.scalar.activation(gT[:, f, :], two(G0)[:, k, :], ACT.Gelu,
                                                bias=col["L1_gnn_b1"][:, f:f + 1])
                last.then_inc(gT_ready, 1)

            all_graphs({"x0": x0, "q0": q0, "k0": k0, "v0": v0, "R0": R0, "S0": S0_, "T0": T0_, "o0": o0,
                        "N0": N0, "x1": x1_, "q1": q1, "k1": k1, "S1": S1_, "T1": T1_,
                        "V1": V1_, "X1": X1, "F1": F1}, act.Fori)

        @block.vector
        def _(dve):
            dve.wait_ge(weights_loaded, 16 * len(wide))

            def stats(key, n, tile):
                st, mv, ve, _ = ln[key]
                stats_done, moments_done, var_ready, _ = ln_sem[key]
                for t in range(T):
                    last = nc.vector.bn_stats(st[:, t, :], tile[:, t, :])
                last.then_inc(stats_done, 1)
                dve.wait_ge(stats_done, n + 1)
                at = U + list(ln).index(key)
                nc.vector.memset(held[:, at:at + 1], 0.0)
                for t in range(T):
                    last = nc.vector.bn_aggr(mv[:, t, :], st[:, t, :])
                last.then_inc(moments_done, 1)
                dve.wait_ge(moments_done, n + 1)
                nc.vector.tensor_scalar_add(ve[:, :], mv[:, :, 1], EPS).then_inc(var_ready, 1)

            def normalise(key, n, dst, src, done):
                _, mv, _, rs = ln[key]
                dve.wait_ge(ln_sem[key][3], n + 1)
                for t in range(T):
                    last = nc.vector.tensor_scalar(dst[:, t, :], src[:, t, :], mv[:, t, 0:1], rs[:, t:t + 1],
                                                   ALU.subtract, ALU.mult)
                last.then_inc(done, 1)

            def low(dst, bank_, high, bias=None):
                if bias is None:
                    return nc.vector.tensor_tensor(dst[:, :, :], two(bank_), high[:, :, :].bitcast(F32), ALU.subtract)
                for c in range(C):
                    last = nc.vector.scalar_tensor_tensor(dst[:, c, :], two(bank_)[:, c, :], bias[:, c:c + 1],
                                                          high[:, c, :].bitcast(F32), ALU.add, ALU.subtract)
                return last

            def q0(n):
                dve.wait_ge(qh0_ready, n + 1)
                low(ql0, S0, qh0).then_inc(q0_ready, 1)

            def k0(n):
                dve.wait_ge(kh0_ready, n + 1)
                low(kl0, T0, kh0).then_inc(k0_ready, 1)

            def q1(n):
                dve.wait_ge(qh1_ready, n + 1)
                low(ql1, S1, qh1, bqs).then_inc(q1_ready, 1)

            def k1(n):
                dve.wait_ge(kh1_ready, n + 1)
                low(kl1, G1, kh1, col["L1_gnn_bk"]).then_inc(k1_ready, 1)

            def m0(n):
                dve.wait_ge(adj_loaded, 16 * (n + 1))
                nc.vector.tensor_scalar(negm[:, :, :], adj_in[:, :, :], 0.0, NEG, ALU.is_le, ALU.mult)\
                    .then_inc(negm_ready, 1)

            def adj0(n):
                if later(n):
                    dve.wait_ge(adjT_psum, n)
                nc.vector.tensor_copy(adjb[:, :, :], adj_in[:, :, :]).then_inc(adjb_ready, 1)

            def S0_(n, u):
                dve.wait_ge(relu0_ready, n * U + u + 1)
                nc.vector.memset(held[:, u:u + 1], 0.0)
                for k in range(2):
                    pb = P0[:, u % 2, k, :]
                    last = nc.vector.tensor_tensor_reduce(out=pb, in0=two(S0)[:, k, :], in1=pb,
                                                          scale=-1.0, scalar=BIG, op0=ALU.add, op1=ALU.min,
                                                          accum_out=nb0[:, u, k:k + 1])
                last.then_inc(leaky0_ready, 1)

            def O0_(n):
                dve.wait_ge(exp0_ready, n * U + U)
                nc.vector.reciprocal(rinv0[:, :, :], sum0[:, :, :]).then_inc(rinv0_ready, 1)
                dve.wait_ge(rinv0_ready, n + 1)
                dve.wait_ge(o0_psum, n + 1)
                if later(n):
                    dve.wait_ge(x1_ready, n)
                nc.vector.tensor_tensor(h0[:, :, :].rearrange("p t (h d) -> p (t h) d", d=DH),
                                        S0[:, :].rearrange("p (a d) -> p a d", d=DH),
                                        rinv0[:, :, :].rearrange("p t (h o) -> p (t h) o", o=1).to_broadcast([P, T * H, DH]),
                                        ALU.mult).then_inc(h0_ready, 1)
                dve.wait_ge(h0_ready, n + 1)
                stats("a0", n, h0)

            def N0(n):
                normalise("a0", n, h0, h0, z0_ready)

            def F0(n):
                dve.wait_ge(ffn0_psum, n * T + T)
                stats("b0", n, two(S0))

            def Y0(n):
                dve.wait_ge(zT0_psum, n + 1)
                normalise("b0", n, y0, two(S0), y0_ready)

            def m1(n):
                dve.wait_ge(adjT_psum, n + 1)
                aT = O1[:, 0:N].bitcast(BF16).rearrange("p (j i) -> p j i", j=T)
                for r in range(R):
                    last = nc.vector.tensor_scalar(M1[:, r, :, :], aT, float(r), None, ALU.is_equal)
                last.then_inc(mask_ready, 1)

            def v1(n, r):
                dve.wait_ge(v1_psum, n * R + r + 1)
                nc.vector.tensor_tensor(V1[:, r, :, :], two([O1, T1][r % 2]), bv[:, r, :, :].to_broadcast([P, T, D]),
                                        ALU.add).then_inc(v1_ready, 1)

            def S1_(n, u):
                dve.wait_ge(scores1, n * U + u + 1)
                nc.vector.tensor_reduce(nb1[:, u, :], two([S1, G1][u % 2]), AX.X, ALU.max, negate=True)\
                    .then_inc(bias1_ready, 1)

            def T1_(n, u):
                c, q, t = unit(u)
                dve.wait_ge(PT1_ready, n * U + u + 1)
                if u == 0:
                    dve.wait_ge(mask_ready, n + 1)
                for r in range(R - 1):
                    if u == 4:
                        dve.wait_ge(av1_psum, n * C * R + r + 1)
                    last = by_relation(nc.vector, u, r)
                last.then_inc(A1_ready, 1)

            def V1_(n):
                dve.wait_ge(exp1_ready, n * U + U)
                nc.vector.reciprocal(rinv1[:, :, 0], sum1[:, :, :].rearrange("p t h -> p (t h)"))\
                    .then_inc(rinv1_ready, 1)
                dve.wait_ge(rinv1_ready, n + 1)
                if later(n):
                    dve.wait_ge(x2T_psum, n)
                    dve.wait_ge(n1g_ready, n)
                nc.vector.tensor_copy(rsp1[:, :, :].rearrange("p t (h d) -> p (t h) d", d=DH),
                                      rinv1[:, :, :].to_broadcast([P, T * H, DH])).then_inc(rsp1_ready, 1)

            def W1(n):
                dve.wait_ge(oT1_ready, n + 1)
                dve.wait_ge(rT1_psum, n + 1)
                nc.vector.tensor_tensor(at1[:, :, :], two(G0), oT1[:, :, :], ALU.mult).then_inc(at1_ready, 1)

            def r1_(n):
                dve.wait_ge(wo1_psum, n + 1)
                dve.wait_ge(x1b_ready, n + 1)
                nc.vector.tensor_tensor(r1[:, :, :], two(G0), x1b[:, :, :], ALU.add).then_inc(r1_ready, 1)
                dve.wait_ge(r1_ready, n + 1)
                stats("a1", n, r1)

            def X1(n):
                normalise("a1", n, r1, r1, n1_ready)

            def r2_(n):
                dve.wait_ge(down_psum, (n + 1) * 2 * T)
                dve.wait_ge(x2b_ready, n + 1)
                if later(n):
                    dve.wait_ge(out_stored, 16 * n)
                nc.vector.tensor_tensor(r2[:, :, :], two(G0), x2b[:, :, :], ALU.add).then_inc(r2_ready, 1)
                dve.wait_ge(r2_ready, n + 1)
                stats("b1", n, r2)

            def Y1(n):
                normalise("b1", n, r2, r2, n2_ready)

            all_graphs({"m0": m0, "adj0": adj0, "q0": q0, "k0": k0, "S0": S0_, "O0": O0_, "N0": N0, "F0": F0,
                        "Y0": Y0, "m1": m1, "q1": q1, "k1": k1, "v1": v1, "S1": S1_, "T1": T1_, "V1": V1_,
                        "W1": W1, "r1": r1_, "X1": X1, "r2": r2_, "Y1": Y1}, dve.Fori)

        @block.tensor
        def _(pe):
            pe.wait_ge(ident_ready, 1)
            pe.wait_ge(weights_loaded, 16 * len(wide))
            for o in range(2 * C):
                if o >= 2:
                    pe.wait_ge(wf_ready, o - 1)
                for c in range(C):
                    last = nc.tensor.transpose([S0, G0][o % 2][:, P * c:P * c + P],
                                               wf0_in[:, c, P * o:P * o + P], ident[:, :])
                last.then_inc(wfT_psum, 1)
            pe.wait_ge(wf_ready, 2 * C)
            pe.wait_ge(identb_ready, 1)

            def mm(out_, lhsT, rhs, start, stop):
                return nc.tensor.matmul(out_, lhsT, rhs, start=start, stop=stop)

            def flip(bank_, tile):
                for a in range(2):
                    for b in range(2):
                        last = nc.tensor.transpose(two(bank_)[:, a, P * b:P * b + P],
                                                   tile[:, b, P * a:P * a + P], ident[:, :])
                return last

            def channels(bank_, weight, xT, cols=0):
                for o in range(2):
                    for c in range(C):
                        last = mm(two(bank_)[:, o, :], weight[:, c, cols + P * o:cols + P * o + P], xT[:, c, :],
                                  c == 0, c == C - 1)
                return last

            def nodes(bank_, pairs, chunks_=range(T)):
                for t in chunks_:
                    for k, (xT, weight) in enumerate(pairs):
                        last = mm(two(bank_)[:, t, :], xT[:, P * t:P * t + P], weight, k == 0, k == len(pairs) - 1)
                return last

            def x0(n):
                pe.wait_ge(x_loaded, 16 * (n + 1))
                if later(n):
                    pe.wait_ge(zf0_ready, n)
                flip(T0, x_in).then_inc(xT0_psum, 1)

            def q0(n):
                pe.wait_ge(xT0_ready, n + 1)
                if later(n):
                    pe.wait_ge(y0_ready, n)
                channels(S0, wq0, xT0).then_inc(q0_psum, 1)

            def k0(n):
                pe.wait_ge(xT0_ready, n + 1)
                channels(T0, wk0, xT0).then_inc(k0_psum, 1)

            def v0(n):
                pe.wait_ge(xT0_ready, n + 1)
                if later(n):
                    pe.wait_ge(oT0_ready, n)
                nodes(O0, [(xT0[:, c, :], wv0[:, c, :]) for c in range(C)]).then_inc(v0_psum, 1)

            def R0(n, u):
                c, q, t = unit(u)
                if u == 0:
                    pe.wait_ge(q0_ready, n + 1)
                    pe.wait_ge(k0_ready, n + 1)
                    pe.wait_ge(negm_ready, n + 1)
                else:
                    pe.wait_ge(leaky0_ready, n * U + u)
                if u in (0, 2):
                    pe.wait_ge(q0_stacked[u // 2], (n + 1) * STACKS)
                    pe.wait_ge(k0_stacked[u // 2], (n + 1) * STACKS)
                mm(two(S0), identb[:, :], negm[:, t:t + 1, :].to_broadcast([P, 2, N]), True, False)
                for k in range(2):
                    last = mm(two(S0)[:, k, :], Qs0[:, q + k, c, P * t:P * t + P], Ks0[:, q + k, c, :], False, k == 1)
                last.then_inc(scores0, 1)

            def blocks(bank_, probs):
                for k in range(2):
                    for j in range(T):
                        at = P * (T * k + j)
                        last = nc.tensor.transpose(bank_[:, at:at + P], probs[:, k, P * j:P * j + P], ident[:, :])
                return last

            def T0_(n, u):
                pe.wait_ge(exp0_ready, n * U + u + 1)
                if u:
                    pe.wait_ge(PT0_ready, n * U + u)
                blocks(T0, P0[:, u % 2, :, :]).then_inc(pT0_psum, 1)

            def A0(n, c):
                pe.wait_ge(PT0_ready, n * U + 4 * c + 4)
                if c == 0:
                    pe.wait_ge(v0_ready, n + 1)
                for j in range(T):
                    for q in range(Q):
                        h = Q * c + q
                        last = mm(two(O0)[DH * q:DH * q + DH, c, :], V0[:, j, DH * h:DH * h + DH],
                                  PT0[:, q, j, :], j == 0, j == T - 1)
                last.then_inc(av0_psum, 1)

            def o0(n):
                pe.wait_ge(oT0_ready, n + 1)
                pe.wait_ge(leaky0_ready, n * U + U)
                flip(S0, oT0).then_inc(o0_psum, 1)

            def N0(n):
                pe.wait_ge(z0_ready, n + 1)
                pe.wait_ge(PT0_ready, n * U + U)
                flip(T0, h0).then_inc(zT0_psum, 1)

            def L0(n, t):
                if t == 0:
                    pe.wait_ge(zf0_ready, n + 1)
                    pe.wait_ge(h0_ready, n + 1)
                last = nodes(S0, [(zf0[:, c, :], wf0[:, c, :]) for c in range(C)] +
                             [(xT0[:, c, :], wf0[:, C + c, :]) for c in range(C)], [t])
                last.then_inc(ffn0_psum, 1)

            def x1_(n):
                pe.wait_ge(x1_ready, n + 1)
                if later(n):
                    pe.wait_ge(PT1_ready, n * U)
                flip(T1, x1).then_inc(xT1_psum, 1)

            def m1(n):
                pe.wait_ge(adjb_ready, n + 1)
                if later(n):
                    pe.wait_ge(oT1_ready, n)
                ob = O1[:, 0:N].bitcast(BF16)
                for j in range(T):
                    for t in range(T):
                        at = N * j + P * t
                        last = nc.tensor.transpose(ob[:, at:at + P], adjb[:, t, P * j:P * j + P], identb[:, :])
                last.then_inc(adjT_psum, 1)

            def q1(n):
                pe.wait_ge(xT1_ready, n + 1)
                if later(n):
                    pe.wait_ge(exp1_ready, n * U - 1)
                channels(S1, wq1, xT1).then_inc(q1_psum, 1)

            def k1(n):
                pe.wait_ge(xT1_ready, n + 1)
                if later(n):
                    pe.wait_ge(exp1_ready, n * U)
                channels(G1, wk1, xT1).then_inc(k1_psum, 1)

            def v1(n, r):
                if r == 0:
                    pe.wait_ge(mask_ready, n + 1)
                elif r == 1:
                    pe.wait_ge(xT1_ready, n + 1)
                else:
                    pe.wait_ge(v1_ready, n * R + r - 1)
                nodes([O1, T1][r % 2], [(xT1[:, c, :], wv1[:, r, c, :]) for c in range(C)]).then_inc(v1_psum, 1)

            def S1_(n, u):
                c, q, t = unit(u)
                if u == 0:
                    pe.wait_ge(q1_ready, n + 1)
                    pe.wait_ge(k1_ready, n + 1)
                if u in (0, 2):
                    pe.wait_ge(q1_stacked[u // 2], (n + 1) * STACKS)
                    pe.wait_ge(k1_stacked[u // 2], (n + 1) * STACKS)
                if u >= 2:
                    pe.wait_ge(exp1_ready, n * U + u - 1)
                for k in range(2):
                    last = mm(two([S1, G1][u % 2])[:, k, :], Qs1[:, q + k, c, P * t:P * t + P], Ks1[:, q + k, c, :],
                              True, True)
                last.then_inc(scores1, 1)

            def T1_(n, u):
                pe.wait_ge(exp1_ready, n * U + u + 1)
                if u:
                    pe.wait_ge(PT1_ready, n * U + u)
                else:
                    pe.wait_ge(v1_ready, n * R + R)
                blocks(T1, P1[:, u % 2, :, :]).then_inc(pT1_psum, 1)

            def A1_(n, c, r):
                if r == 0:
                    pe.wait_ge(A1_ready, n * U + 4 * c + 4)
                elif r == R - 1:
                    pe.wait_ge(A13_ready, n * U + 4 * c + 4)
                if c == 0 and r == 0:
                    pe.wait_ge(v1_ready, n * R + R)
                for j in range(T):
                    for q in range(Q):
                        h = Q * c + q
                        last = mm(two(O1)[DH * q:DH * q + DH, c, :], V1[:, r, j, DH * h:DH * h + DH],
                                  A1[:, r, q, j, :], r == 0 and j == 0, r == R - 1 and j == T - 1)
                last.then_inc(av1_psum, 1)

            def Z1(n):
                pe.wait_ge(rsp1_ready, n + 1)
                if later(n):
                    pe.wait_ge(r2_ready, n)
                flip(G0, rsp1).then_inc(rT1_psum, 1)

            def W1(n):
                pe.wait_ge(at1_ready, n + 1)
                nodes(G0, [(at1[:, c, :], wo1[:, c, :]) for c in range(C)]).then_inc(wo1_psum, 1)

            def X1(n):
                pe.wait_ge(r1_ready, n + 1)
                pe.wait_ge(n1_ready, n + 1)
                flip(G0, r1).then_inc(x2T_psum, 1)

            def F1(n, g):
                if g == 0:
                    pe.wait_ge(x2T_ready, n + 1)
                else:
                    pe.wait_ge(gT_ready, n * FB + g)
                channels(G0, w1, x2T, cols=2 * P * g).then_inc(up_psum, 1)

            def F2(n, k):
                if k == 0:
                    pe.wait_ge(gT_ready, n * FB + FB)
                t, first = k // 2, k % 2 * FB
                for f in range(first, first + FB):
                    last = mm(two(G0)[:, t, :], gT[:, f, P * t:P * t + P], w2[:, f, :], f == 0, f == FC - 1)
                last.then_inc(down_psum, 1)

            all_graphs({"x0": x0, "q0": q0, "k0": k0, "v0": v0, "R0": R0, "T0": T0_, "A0": A0, "o0": o0,
                            "N0": N0, "L0": L0, "x1": x1_, "m1": m1, "q1": q1, "k1": k1, "v1": v1, "S1": S1_,
                            "T1": T1_, "A1": A1_, "Z1": Z1, "W1": W1, "X1": X1, "F1": F1, "F2": F2}, pe.Fori)


WEIGHTS = ["L0_gnn_Wq", "L0_gnn_Wk", "L0_gnn_Wv", "L0_gnn_Wffn", "L0_gnn_g1", "L0_gnn_b1", "L0_gnn_g2",
           "L0_gnn_b2", "L1_gnn_Wq", "L1_gnn_bq", "L1_gnn_Wk", "L1_gnn_bk", "L1_gnn_Wv", "L1_gnn_bv",
           "L1_gnn_Wo", "L1_gnn_bo", "L1_gnn_W1", "L1_gnn_b1", "L1_gnn_W2", "L1_gnn_b2", "L1_gnn_g1",
           "L1_gnn_beta1", "L1_gnn_g2", "L1_gnn_beta2"]


def kernel(**inputs):
    import numpy as _np
    import concourse.bacc as _bacc
    from concourse import mybir as _mybir
    from concourse.bass_utils import run_bass_kernel_spmd as _run

    nc = _bacc.Bacc("TRN2", target_bir_lowering=False, num_devices=1)
    arrays, aps = {}, {}
    for name in ["x", "adj"] + WEIGHTS:
        a = _np.ascontiguousarray(inputs[name])
        arrays[f"in_{name}"] = a
        aps[name] = nc.dram_tensor(f"in_{name}", a.shape, _mybir.dt.from_np(a.dtype), kind="ExternalInput").ap()
    out = nc.dram_tensor("out_x", arrays["in_x"].shape, _mybir.dt.float32, kind="ExternalOutput").ap()
    graph_layers_kernel(nc, aps["x"], aps["adj"], {name: aps[name] for name in WEIGHTS}, out)
    r = _run(nc, [arrays], core_ids=[0])
    return r.results[0]["out_x"]
```
